# Optimizing a Trainium2 kernel written in Bass

```python
import numpy as np
import jax
import jax.numpy as jnp

def _softmax(x, axis=-1):
    return jax.nn.softmax(x, axis=axis)

def _gelu(x):
    return jax.nn.gelu(x, approximate=True)

def _silu(x):
    return jax.nn.silu(x)

def _sigmoid(x):
    return jax.nn.sigmoid(x)

def _layernorm(x, axis=-1, eps=1e-05):
    m = jnp.mean(x, axis=axis, keepdims=True)
    v = jnp.var(x, axis=axis, keepdims=True)
    return (x - m) / jnp.sqrt(v + eps)

def _scatter_add(tgt, idx, src, axis=0):
    return tgt.at[idx].add(src)

def _segment_sum(src, seg, n):
    return jax.ops.segment_sum(src, seg, n)
kernel_name = 'mk_macaron_d1_jaxref_r8_aa4001'

def setup_inputs(seed: int=0):
    np.random.seed(seed)
    _w = jnp.asarray

    def _L0_attn_setup():
        import jax, jax.numpy as jnp
        import numpy as np
        B, T, D = (8, 256, 128)
        FF = 4 * D
        EPS = 1e-05

        def layer_norm(x, g, b):
            mu = jnp.mean(x, axis=-1, keepdims=True)
            var = jnp.var(x, axis=-1, keepdims=True)
            return (x - mu) * jax.lax.rsqrt(var + EPS) * g + b

        def token_shift(x):
            return jnp.pad(x, ((0, 0), (1, 0), (0, 0)))[:, :-1]

        def wkv_scan(k, v, time_decay, time_first):
            w = -jnp.exp(time_decay)
            u = time_first

            def step(carry, kv):
                aa, bb, pp = carry
                kt, vt = kv
                ww = u + kt
                p = jnp.maximum(pp, ww)
                e1 = jnp.exp(pp - p)
                e2 = jnp.exp(ww - p)
                out = (e1 * aa + e2 * vt) / (e1 * bb + e2)
                ww2 = pp + w
                p2 = jnp.maximum(ww2, kt)
                e1b = jnp.exp(ww2 - p2)
                e2b = jnp.exp(kt - p2)
                return ((e1b * aa + e2b * vt, e1b * bb + e2b, p2), out)
            z = jnp.zeros((k.shape[0], k.shape[2]), k.dtype)
            init = (z, z, jnp.full_like(z, -1e+38))
            _, outs = jax.lax.scan(step, init, (jnp.moveaxis(k, 1, 0), jnp.moveaxis(v, 1, 0)))
            return jnp.moveaxis(outs, 0, 1)
        key = jax.random.key(seed)
        ks = jax.random.split(key, 20)
        rn = lambda k, s, sc=0.02: jax.random.normal(k, s, jnp.float32) * sc
        return {'x': jax.random.normal(ks[0], (B, T, D), jnp.float32), 'ln1_g': jnp.ones((D,), jnp.float32), 'ln1_b': jnp.zeros((D,), jnp.float32), 'ln2_g': jnp.ones((D,), jnp.float32), 'ln2_b': jnp.zeros((D,), jnp.float32), 'tm_mix_k': jax.random.uniform(ks[1], (D,), jnp.float32), 'tm_mix_v': jax.random.uniform(ks[2], (D,), jnp.float32), 'tm_mix_r': jax.random.uniform(ks[3], (D,), jnp.float32), 'time_decay': rn(ks[4], (D,), 1.0), 'time_first': rn(ks[5], (D,), 0.5), 'wk': rn(ks[6], (D, D)), 'wv': rn(ks[7], (D, D)), 'wr': rn(ks[8], (D, D)), 'wo': rn(ks[9], (D, D)), 'cm_mix_k': jax.random.uniform(ks[10], (D,), jnp.float32), 'cm_mix_r': jax.random.uniform(ks[11], (D,), jnp.float32), 'cwk': rn(ks[12], (D, FF)), 'cwv': rn(ks[13], (FF, D)), 'cwr': rn(ks[14], (D, D))}
    _L0_attn_in = _L0_attn_setup()

    def _L0_ffn_setup():
        import jax, jax.numpy as jnp
        import numpy as np
        E = 16
        H = 128
        F = 256
        TOP_K = 1
        B, S = (2, 128)
        key = jax.random.key(seed)
        ks = jax.random.split(key, 7)
        s = 0.02
        return {'hidden_states': jax.random.normal(ks[0], (B, S, H), jnp.float32), 'w_router': jax.random.normal(ks[1], (E, H), jnp.float32) * s, 'gate_up_proj': jax.random.normal(ks[2], (E, H, 2 * F), jnp.float32) * s, 'down_proj': jax.random.normal(ks[3], (E, F, H), jnp.float32) * s, 'w_gate': jax.random.normal(ks[4], (F, H), jnp.float32) * s, 'w_up': jax.random.normal(ks[5], (F, H), jnp.float32) * s, 'w_down': jax.random.normal(ks[6], (H, F), jnp.float32) * s}
    _L0_ffn_in = _L0_ffn_setup()
    _d = {'L0_attn_x': _L0_attn_in['x'], 'L0_attn_ln1_g': _L0_attn_in['ln1_g'], 'L0_attn_ln1_b': _L0_attn_in['ln1_b'], 'L0_attn_ln2_g': _L0_attn_in['ln2_g'], 'L0_attn_ln2_b': _L0_attn_in['ln2_b'], 'L0_attn_tm_mix_k': _L0_attn_in['tm_mix_k'], 'L0_attn_tm_mix_v': _L0_attn_in['tm_mix_v'], 'L0_attn_tm_mix_r': _L0_attn_in['tm_mix_r'], 'L0_attn_time_decay': _L0_attn_in['time_decay'], 'L0_attn_time_first': _L0_attn_in['time_first'], 'L0_attn_wk': _L0_attn_in['wk'], 'L0_attn_wv': _L0_attn_in['wv'], 'L0_attn_wr': _L0_attn_in['wr'], 'L0_attn_wo': _L0_attn_in['wo'], 'L0_attn_cm_mix_k': _L0_attn_in['cm_mix_k'], 'L0_attn_cm_mix_r': _L0_attn_in['cm_mix_r'], 'L0_attn_cwk': _L0_attn_in['cwk'], 'L0_attn_cwv': _L0_attn_in['cwv'], 'L0_attn_cwr': _L0_attn_in['cwr'], 'L0_ffn_w_router': _L0_ffn_in['w_router'], 'L0_ffn_gate_up_proj': _L0_ffn_in['gate_up_proj'], 'L0_ffn_down_proj': _L0_ffn_in['down_proj'], 'L0_ffn_w_gate': _L0_ffn_in['w_gate'], 'L0_ffn_w_up': _L0_ffn_in['w_up'], 'L0_ffn_w_down': _L0_ffn_in['w_down']}
    _x0 = _d['L0_attn_x']
    _d['L0_attn_x'] = jax.random.normal(jax.random.fold_in(jax.random.key(seed), 1), (4, 512, 128), dtype=_x0.dtype)
    del _x0
    return _d

def reference(L0_attn_x, L0_attn_ln1_g, L0_attn_ln1_b, L0_attn_ln2_g, L0_attn_ln2_b, L0_attn_tm_mix_k, L0_attn_tm_mix_v, L0_attn_tm_mix_r, L0_attn_time_decay, L0_attn_time_first, L0_attn_wk, L0_attn_wv, L0_attn_wr, L0_attn_wo, L0_attn_cm_mix_k, L0_attn_cm_mix_r, L0_attn_cwk, L0_attn_cwv, L0_attn_cwr, L0_ffn_w_router, L0_ffn_gate_up_proj, L0_ffn_down_proj, L0_ffn_w_gate, L0_ffn_w_up, L0_ffn_w_down):

    def _L0_attn_ref(x, ln1_g, ln1_b, ln2_g, ln2_b, tm_mix_k, tm_mix_v, tm_mix_r, time_decay, time_first, wk, wv, wr, wo, cm_mix_k, cm_mix_r, cwk, cwv, cwr):
        import jax, jax.numpy as jnp
        import numpy as np
        B, T, D = (8, 256, 128)
        FF = 4 * D
        EPS = 1e-05

        def layer_norm(x, g, b):
            mu = jnp.mean(x, axis=-1, keepdims=True)
            var = jnp.var(x, axis=-1, keepdims=True)
            return (x - mu) * jax.lax.rsqrt(var + EPS) * g + b

        def token_shift(x):
            return jnp.pad(x, ((0, 0), (1, 0), (0, 0)))[:, :-1]

        def wkv_scan(k, v, time_decay, time_first):
            w = -jnp.exp(time_decay)
            u = time_first

            def step(carry, kv):
                aa, bb, pp = carry
                kt, vt = kv
                ww = u + kt
                p = jnp.maximum(pp, ww)
                e1 = jnp.exp(pp - p)
                e2 = jnp.exp(ww - p)
                out = (e1 * aa + e2 * vt) / (e1 * bb + e2)
                ww2 = pp + w
                p2 = jnp.maximum(ww2, kt)
                e1b = jnp.exp(ww2 - p2)
                e2b = jnp.exp(kt - p2)
                return ((e1b * aa + e2b * vt, e1b * bb + e2b, p2), out)
            z = jnp.zeros((k.shape[0], k.shape[2]), k.dtype)
            init = (z, z, jnp.full_like(z, -1e+38))
            _, outs = jax.lax.scan(step, init, (jnp.moveaxis(k, 1, 0), jnp.moveaxis(v, 1, 0)))
            return jnp.moveaxis(outs, 0, 1)
        h = layer_norm(x, ln1_g, ln1_b)
        hx = token_shift(h)
        k = jnp.einsum('btd,de->bte', h * tm_mix_k + hx * (1.0 - tm_mix_k), wk)
        v = jnp.einsum('btd,de->bte', h * tm_mix_v + hx * (1.0 - tm_mix_v), wv)
        r = jax.nn.sigmoid(jnp.einsum('btd,de->bte', h * tm_mix_r + hx * (1.0 - tm_mix_r), wr))
        wkv = wkv_scan(k, v, time_decay, time_first)
        x = x + jnp.einsum('btd,de->bte', r * wkv, wo)
        h = layer_norm(x, ln2_g, ln2_b)
        hx = token_shift(h)
        kk = jnp.einsum('btd,df->btf', h * cm_mix_k + hx * (1.0 - cm_mix_k), cwk)
        kk = jnp.square(jax.nn.relu(kk))
        rr = jax.nn.sigmoid(jnp.einsum('btd,de->bte', h * cm_mix_r + hx * (1.0 - cm_mix_r), cwr))
        x = x + rr * jnp.einsum('btf,fd->btd', kk, cwv)
        return x

    def _L0_ffn_ref(hidden_states, w_router, gate_up_proj, down_proj, w_gate, w_up, w_down):
        import jax, jax.numpy as jnp
        import numpy as np
        E = 16
        H = 128
        F = 256
        TOP_K = 1
        B, S = (2, 128)
        b, s, h = hidden_states.shape
        x = hidden_states.reshape(-1, h)
        logits = x @ w_router.T
        _, top_idx = jax.lax.top_k(logits, TOP_K)
        mask = jax.nn.one_hot(top_idx, E, dtype=logits.dtype).sum(axis=1)
        scores = jax.nn.sigmoid(logits) * mask
        masked_inputs = scores.T[:, :, None] * x[None, :, :]
        gate_up = jnp.einsum('eth,ehf->etf', masked_inputs, gate_up_proj)
        gate, up = jnp.split(gate_up, 2, axis=-1)
        expert_out = jnp.einsum('etf,efh->eth', up * jax.nn.silu(gate), down_proj)
        shared = jax.nn.silu(x @ w_gate.T) * (x @ w_up.T) @ w_down.T
        out = shared + expert_out.sum(axis=0)
        return out.reshape(b, s, h)
    x = L0_attn_x
    x = x + 0.5 * _L0_ffn_ref(_layernorm(x, axis=-1), L0_ffn_w_router, L0_ffn_gate_up_proj, L0_ffn_down_proj, L0_ffn_w_gate, L0_ffn_w_up, L0_ffn_w_down)
    x = x + _L0_attn_ref(_layernorm(x, axis=-1), L0_attn_ln1_g, L0_attn_ln1_b, L0_attn_ln2_g, L0_attn_ln2_b, L0_attn_tm_mix_k, L0_attn_tm_mix_v, L0_attn_tm_mix_r, L0_attn_time_decay, L0_attn_time_first, L0_attn_wk, L0_attn_wv, L0_attn_wr, L0_attn_wo, L0_attn_cm_mix_k, L0_attn_cm_mix_r, L0_attn_cwk, L0_attn_cwv, L0_attn_cwr)
    x = x + 0.5 * _L0_ffn_ref(_layernorm(x, axis=-1), L0_ffn_w_router, L0_ffn_gate_up_proj, L0_ffn_down_proj, L0_ffn_w_gate, L0_ffn_w_up, L0_ffn_w_down)
    return x

_drawn_inputs = setup_inputs


def setup_inputs(seed=0):
    import zlib

    import numpy as np

    out = dict(_drawn_inputs(seed))
    spreads = {'L0_attn_ln1_g': (1.0, 0.6),
     'L0_attn_ln1_b': (0.0, 0.8),
     'L0_attn_ln2_g': (1.0, 0.6),
     'L0_attn_ln2_b': (0.0, 0.8)}
    factors = {'L0_attn_tm_mix_k': 8.0,
     'L0_attn_tm_mix_v': 8.0,
     'L0_attn_tm_mix_r': 8.0,
     'L0_attn_time_decay': 8.0,
     'L0_attn_time_first': 8.0,
     'L0_attn_wk': 8.0,
     'L0_attn_wv': 7.765,
     'L0_attn_wr': 8.0,
     'L0_attn_wo': 7.893,
     'L0_attn_cm_mix_k': 8.0,
     'L0_attn_cm_mix_r': 8.0,
     'L0_attn_cwk': 8.0,
     'L0_attn_cwv': 8.0,
     'L0_attn_cwr': 8.0,
     'L0_ffn_w_router': 8.0,
     'L0_ffn_gate_up_proj': 8.0,
     'L0_ffn_down_proj': 8.0,
     'L0_ffn_w_gate': 8.0,
     'L0_ffn_w_up': 8.0,
     'L0_ffn_w_down': 8.0}
    for name, (base, spread) in spreads.items():
        noise = np.random.default_rng([zlib.crc32(name.encode()), seed]).standard_normal(out[name].shape)
        drawn = base * np.exp(spread * noise) if base else spread * noise
        out[name] = jnp.asarray(drawn.astype(out[name].dtype))
    for name, factor in factors.items():
        out[name] = (out[name] * factor).astype(out[name].dtype)
    return out
```

```python
from contextlib import ExitStack

import concourse.bass as bass
from concourse import mybir

ALU = mybir.AluOpType
ACT = mybir.ActivationFunctionType
AX = mybir.AxisListType
F32 = mybir.dt.float32
BF16 = mybir.dt.bfloat16
I32 = mybir.dt.int32

P = 128
EPS = 1e-5
ROUND = float(2 ** 23)
LOWEST = -1e38


def macaron_kernel(nc, t_in, out):
    x_in = t_in["L0_attn_x"]
    NB, T, D = x_in.shape
    assert D == P and T % P == 0
    J = T // P
    NT = NB * J
    E, _, F2 = t_in["L0_ffn_gate_up_proj"].shape
    FM = F2 // 2
    FC = FM // P
    FS = t_in["L0_ffn_w_gate"].shape[0]
    SC = FS // P
    CF = t_in["L0_attn_cwk"].shape[1]
    CC = CF // P
    NBLK = NT + E - 1
    WMIX = ("k", "v", "r")
    KD = 2

    ctx = ExitStack()
    with ctx:
        def sb(name, shape, dt=F32):
            return ctx.enter_context(nc.sbuf_tensor(name, shape, dt))

        def sem(name):
            return ctx.enter_context(nc.semaphore(name))

        bank = [ctx.enter_context(nc.psum_tensor(f"bank{i}", [P, 512], F32)) for i in range(8)]

        slots_dram = nc.dram_tensor("slots_dram", [NBLK * P, D], F32, kind="Internal").ap()
        moe_dram = nc.dram_tensor("moe_dram", [NBLK * P, D], F32, kind="Internal").ap()

        gate_up = sb("gate_up", [P, E, F2])
        down = sb("down", [P, E, FC, D])
        w_gate_raw = sb("w_gate_raw", [P, SC, D])
        w_up_raw = sb("w_up_raw", [P, SC, D])
        w_down_raw = sb("w_down_raw", [P, FS])
        w_router_raw = sb("w_router_raw", [E, D])
        w_gateT = sb("w_gateT", [P, SC, P])
        w_upT = sb("w_upT", [P, SC, P])
        w_downT = sb("w_downT", [P, SC, D])
        w_routerT = sb("w_routerT", [P, E])
        w_tm = {m: sb(f"w{m}", [P, D]) for m in WMIX}
        w_now = {m: sb(f"w{m}_now", [P, D]) for m in WMIX}
        w_prev = {m: sb(f"w{m}_prev", [P, D]) for m in WMIX}
        wo = sb("wo", [P, D])
        cwk = sb("cwk", [P, CF])
        cwr = sb("cwr", [P, D])
        cwv = sb("cwv", [P, CC, D])
        VEC = ["ln1_g", "ln1_b", "ln2_g", "ln2_b", "tm_mix_k", "tm_mix_v", "tm_mix_r",
               "time_decay", "time_first", "cm_mix_k", "cm_mix_r"]
        vec = {v: sb(v, [P, 1]) for v in VEC}
        one_minus = sb("one_minus", [P, 3])
        decay_exp = sb("decay_exp", [P, 1])
        decay = sb("decay", [P, 1])
        decay_row = sb("decay_row", [P, T])
        ident = sb("ident", [P, P])
        before = sb("before", [P, P], BF16)
        ones = sb("ones", [P, P], BF16)
        rank = sb("rank", [P, E])
        carry = sb("carry", [P, E, NT])
        block_no = sb("block_no", [1, NBLK])
        half_neg = sb("half_neg", [P, 2 * NT])
        ones_row = sb("ones_row", [P, E])
        zero_rows = sb("zero_rows", [P, 8 * D])

        X = sb("X", [P, NT, D])
        xn = sb("xn", [P, NT, D])
        xs = sb("xs", [P, NT, D])
        xnT = sb("xnT", [P, NB, T])
        yg = xs
        stats = sb("stats", [P, NT, 6])
        mv = sb("mv", [P, NT, 2])
        veps = sb("veps", [P, 2 * NT])
        rstd = sb("rstd", [P, 2 * NT])
        best = sb("best", [P, NT])
        th_score = sb("th_score", [P, NT])
        score = sb("score", [P, NT])
        is_best = sb("is_best", [P, NT, E])
        ranked = sb("ranked", [P, NT, E])
        top_rank = sb("top_rank", [P, NT])
        onehot = sb("onehot", [P, NT, E], BF16)
        count = sb("count", [P, E])
        blocks_f = sb("blocks_f", [P, E])
        blocks = sb("blocks", [P, E])
        block_end = sb("block_end", [P, E + 1])
        steps = sb("steps", [P, E, NT])
        tile_start = sb("tile_start", [P, E, NT])
        slot_all = sb("slot_all", [P, NT, E])
        slot_sel = sb("slot_sel", [P, NT, E])
        slot_f = sb("slot_f", [P, NT])
        slot = sb("slot", [P, NT], I32)
        past = sb("past", [1, NBLK, E - 1])
        block_expert_f = sb("block_expert_f", [1, NBLK])
        block_expert = sb("block_expert", [1, NBLK], I32)
        sg = [sb(f"sg{c}", [P, T]) for c in range(SC)]
        act = [sb(f"act{c}", [P, T]) for c in range(SC)]
        NXB = 4
        xb = [sb(f"xb{i}", [P, D]) for i in range(NXB)]
        xbT = [sb(f"xbT{i}", [P, P]) for i in range(2)]
        mg = [sb(f"mg{i}", [P, FM]) for i in range(2)]
        ma = [sb(f"ma{i}", [P, FM]) for i in range(2)]
        maT = [sb(f"maT{i}", [P, FC, P]) for i in range(2)]
        yb = [sb(f"yb{i}", [P, D]) for i in range(NXB)]

        def tiles(ap, b):
            return ap[:, J * b:J * b + J, :]

        def flat(ap, b):
            return ap[:, J * b:J * b + J, :].rearrange("p t d -> p (t d)")

        def two(name, shape):
            return [sb(f"{name}{i}", shape) for i in range(2)]

        a_stats = two("a_stats", [P, J, 6])
        a_mv = two("a_mv", [P, J, 2])
        a_veps = two("a_veps", [P, 2 * J])
        a_rstd = two("a_rstd", [P, 2 * J])
        h1 = [tiles(xn, i) for i in range(2)]
        a_in = [tiles(xn, 2 + i) for i in range(2)]
        x2 = [xnT[:, i, :].rearrange("p (t d) -> p t d", d=D) for i in range(2)]
        h2 = [xnT[:, 2 + i, :].rearrange("p (t d) -> p t d", d=D) for i in range(2)]
        dh = sg
        kk = [zero_rows[:, 0:T], zero_rows[:, T:2 * T], act[0], act[1]]
        h1T = two("h1T", [P, T + 1])
        peak = two("peak", [P, T + 1])
        d_now = two("d_now", [P, T])
        d_old = two("d_old", [P, T])
        d_out = two("d_out", [P, T])
        d_neg = two("d_neg", [P, T])
        d_pos = d_out
        e2b, e1b, e2, e1 = d_now, d_old, d_neg, d_pos
        kv = two("kv", [P, T])
        aa = two("aa", [P, T + 1])
        bb = two("bb", [P, T + 1])
        num_new = two("num_new", [P, T])
        num_old = two("num_old", [P, T])
        den_old = two("den_old", [P, T])
        th_r = two("th_r", [P, T])
        rw = num_new
        c_stats = two("c_stats", [P, J, 6])
        c_mv = two("c_mv", [P, J, 2])
        c_veps = two("c_veps", [P, J])
        c_rstd = two("c_rstd", [P, J])
        h2T = two("h2T", [P, T + 1])
        mix_k = two("mix_k", [P, T])
        mix_r = two("mix_r", [P, T])
        th_rr = two("th_rr", [P, T])

        s_x = [sem(f"s_xin{b}") for b in range(NB)]
        s_wsh = sem("s_wsh")
        s_wmoe = sem("s_wmoe")
        s_watt = sem("s_watt")
        s_zero_set = sem("s_zero_set")
        s_zeroed = sem("s_zeroed")
        s_cmem = sem("s_cmem")
        s_const = sem("s_const")
        s_wtp = sem("s_wtp")
        s_wt = sem("s_wt")
        s_stats = sem("s_stats")
        s_mv = sem("s_mv")
        s_veps = sem("s_veps")
        s_rstd = sem("s_rstd")
        s_xn = sem("s_xn")
        s_xnTp = sem("s_xnTp")
        s_xnT = sem("s_xnT")
        s_logit = sem("s_logit")
        s_best = sem("s_best")
        s_thsc = sem("s_thsc")
        s_score = sem("s_score")
        s_xs = sem("s_xs")
        s_rt = sem("s_rt")
        s_onehot = sem("s_onehot")
        s_count = sem("s_count")
        s_slot = sem("s_slot")
        s_bexp = sem("s_bexp")
        s_scat = sem("s_scat")
        s_sgu = sem("s_sgu")
        s_ssilu = sem("s_ssilu")
        s_sact = sem("s_sact")
        s_sdn = sem("s_sdn")
        s_sres = sem("s_sres")
        s_xb = [sem(f"s_xb{i}") for i in range(NXB)]
        s_xbTp = sem("s_xbTp")
        s_xbT = sem("s_xbT")
        s_mgu = sem("s_mgu")
        s_mg = sem("s_mg")
        s_ma = sem("s_ma")
        s_maTp = sem("s_maTp")
        s_maT = sem("s_maT")
        s_my = sem("s_my")
        s_yb = sem("s_yb")
        s_yst = [sem(f"s_yst{i}") for i in range(NXB)]
        s_yg = [sem(f"s_yg{b}") for b in range(NB)]
        s_x1 = sem("s_x1")
        s_out = sem("s_out")
        ATT = ["a_stats", "a_mv", "a_veps", "a_rstd", "a_norm", "h1Tp", "h1T", "k", "v", "r", "th_r", "peak",
               "d_now", "d_out", "d_old", "d_neg", "d_pos", "e2b", "e1b", "e2", "e1", "kv", "aa", "bb",
               "num_new", "num_old", "den_old", "den", "num", "rden", "wkv", "rw", "wo", "x2", "c_stats",
               "c_mv", "c_veps", "c_rstd", "h2", "h2Tp", "h2T", "dh", "mix_k", "mix_r", "cwk", "pos_kk",
               "kk_d", "kk_g", "rr", "th_rr", "cwv", "x12", "rcv", "x_att"]
        sa = {n: sem("s_" + n + "_a") for n in ATT}
        s_edge = sem("s_edge")
        s_omix = sem("s_omix")
        s_wmix = sem("s_wmix")
        s_dexp = sem("s_dexp")
        s_prep = sem("s_prep")

        x_dram = x_in.rearrange("b (t p) d -> b p t d", p=P)
        out_dram = out.rearrange("b (t p) d -> b p t d", p=P)

        block = ctx.enter_context(nc.Block())

        @block.sync
        def _(sp):
            for b in range(NB):
                sp.dma_start(tiles(X, b), x_dram[b]).then_inc(s_x[b], 16)
                if b == 0:
                    sp.dma_start(w_router_raw[:, :], t_in["L0_ffn_w_router"]).then_inc(s_wsh, 16)
                    sp.dma_start(w_gate_raw[:, :, :], t_in["L0_ffn_w_gate"].rearrange(
                        "(c p) d -> p c d", p=P)).then_inc(s_wsh, 16)
                    sp.dma_start(w_up_raw[:, :, :], t_in["L0_ffn_w_up"].rearrange(
                        "(c p) d -> p c d", p=P)).then_inc(s_wsh, 16)
                    sp.dma_start(w_down_raw[:, :], t_in["L0_ffn_w_down"]).then_inc(s_wsh, 16)
            sp.wait_ge(s_zero_set, 1)
            q = 0
            while q < NBLK * P:
                n = min(8 * P, NBLK * P - q)
                sp.dma_start(slots_dram[q:q + n, :].rearrange("(p r) d -> p (r d)", p=P),
                             zero_rows[:, :n // P * D]).then_inc(s_zeroed, 16)
                q += n
            for e in range(0, E, 4):
                sp.dma_start(gate_up[:, e:e + 4, :], t_in["L0_ffn_gate_up_proj"][e:e + 4].rearrange(
                    "e h f -> h e f")).then_inc(s_wmoe, 16)
                sp.dma_start(down[:, e:e + 4, :, :], t_in["L0_ffn_down_proj"][e:e + 4].rearrange(
                    "e (c p) d -> p e c d", p=P)).then_inc(s_wmoe, 16)
            for v in VEC:
                sp.dma_start(vec[v][:, :], t_in["L0_attn_" + v].rearrange("(p a) -> p a", a=1)
                             ).then_inc(s_watt, 16)
            for m in WMIX:
                sp.dma_start(w_tm[m][:, :], t_in["L0_attn_w" + m]).then_inc(s_watt, 16)
            sp.dma_start(wo[:, :], t_in["L0_attn_wo"]).then_inc(s_watt, 16)
            sp.dma_start(cwk[:, :], t_in["L0_attn_cwk"]).then_inc(s_watt, 16)
            sp.dma_start(cwr[:, :], t_in["L0_attn_cwr"]).then_inc(s_watt, 16)
            sp.dma_start(cwv[:, :, :], t_in["L0_attn_cwv"].rearrange("(c p) d -> p c d", p=P)
                         ).then_inc(s_watt, 16)

            def load_block(n, i):
                sp.dma_start(xb[n % NXB][:, :], slots_dram[bass.ts(i, P), :]).then_inc(s_xb[n % NXB], 16)

            def run_blocks(v):
                sp.wait_ge(s_scat, 16 * NT * (v + 1))
                o = v * NBLK
                for i in range(NXB):
                    if v:
                        sp.wait_ge(s_xbTp, o + i - NXB + 1)
                    load_block(o + i, i)
                loops = (NBLK - NXB) // NXB
                with sp.Fori(0, loops) as r:
                    for k in range(NXB):
                        sp.wait_ge(s_xbTp, r * NXB + (o + k + 1))
                        load_block(o + k, r * NXB + (NXB + k))
                for i in range(NXB * (loops + 1), NBLK):
                    sp.wait_ge(s_xbTp, o + i - NXB + 1)
                    load_block(o + i, i)

            run_blocks(0)
            run_blocks(1)
            for b in range(NB):
                sp.wait_ge(s_x1, NB + b + 1)
                sp.dma_start(out_dram[b], tiles(X, b)).then_inc(s_out, 16)
            sp.wait_ge(s_out, 16 * NB)

        @block.gpsimd
        def _(g):
            g.memset(zero_rows[:, :], 0.0).then_inc(s_zero_set, 1)
            g.memset(ident[:, :], 0.0).then_inc(s_cmem, 1)
            g.memset(before[:, :], 1.0).then_inc(s_cmem, 1)
            g.memset(carry[:, :, :], 1.0).then_inc(s_cmem, 1)
            g.memset(ones[:, :], 1.0).then_inc(s_const, 1)
            g.memset(half_neg[:, :], -0.5).then_inc(s_const, 1)
            g.memset(ones_row[:, :], 1.0).then_inc(s_const, 1)
            g.memset(block_end[:, :], 0.0).then_inc(s_const, 1)
            g.iota(rank[:, :], pattern=[[-1, E]], base=E, channel_multiplier=0,
                   allow_small_or_imprecise_dtypes=True).then_inc(s_const, 1)
            g.iota(block_no[:, :], pattern=[[1, NBLK]], base=0, channel_multiplier=0,
                   allow_small_or_imprecise_dtypes=True).then_inc(s_const, 1)
            g.wait_ge(s_cmem, 3)
            g.affine_select(out=ident[:, :], in_=ident[:, :], compare_op=ALU.not_equal, fill=1.0,
                            base=0, pattern=[[-1, P]], channel_multiplier=1).then_inc(s_const, 1)
            g.affine_select(out=before[:, :], in_=before[:, :], compare_op=ALU.is_gt, fill=0.0,
                            base=0, pattern=[[1, P]], channel_multiplier=-1).then_inc(s_const, 1)
            g.affine_select(out=carry[:, :, :], in_=carry[:, :, :], compare_op=ALU.is_gt, fill=0.0,
                            base=0, pattern=[[0, E], [1, NT]], channel_multiplier=0
                            ).then_inc(s_const, 1)

            def rsqrt_ffn(v):
                for b in range(NB):
                    n = v * NB + b + 1
                    g.wait_ge(s_mv, n)
                    g.tensor_scalar(veps[:, J * b:J * b + J], mv[:, J * b:J * b + J, 1], EPS, None,
                                    ALU.add).then_inc(s_veps, 1)
                    g.wait_ge(s_veps, n)
                    g.tensor_tensor(rstd[:, J * b:J * b + J], veps[:, J * b:J * b + J],
                                    half_neg[:, 0:J], ALU.pow).then_inc(s_rstd, 1)

            def scatter(v):
                if v == 0:
                    g.wait_ge(s_zeroed, 16 * ((NBLK + 7) // 8))
                g.wait_ge(s_slot, v + 1)
                for b in range(NB):
                    g.wait_ge(s_xs, v * NB + b + 1)
                    for t in range(J * b, J * b + J):
                        g.indirect_dma_start(
                            out=slots_dram, out_offset=bass.IndirectOffsetOnAxis(ap=slot[:, t:t + 1], axis=0),
                            in_=xs[:, t, :], in_offset=None).then_inc(s_scat, 16)

            def gather(v):
                for k in range(NXB):
                    g.wait_ge(s_yst[k], 16 * len([i for i in range((v + 1) * NBLK) if i % NXB == k]))
                for t in range(NT):
                    g.indirect_dma_start(
                        out=yg[:, t, :], out_offset=None, in_=moe_dram,
                        in_offset=bass.IndirectOffsetOnAxis(ap=slot[:, t:t + 1], axis=0)
                    ).then_inc(s_yg[t // J], 16)

            def rwkv():
                def rstd_in(b):
                    i, n = b % 2, b + 1
                    g.wait_ge(sa["a_mv"], n)
                    g.tensor_scalar(a_veps[i][:, 0:J], a_mv[i][:, :, 1], EPS, None, ALU.add)
                    g.tensor_scalar(a_veps[i][:, J:2 * J], a_mv[i][:, :, 1], 1.0 + EPS, EPS * EPS,
                                    ALU.mult, ALU.add).then_inc(sa["a_veps"], 1)
                    g.wait_ge(sa["a_veps"], n)
                    if b >= 2:
                        g.wait_ge(sa["a_norm"], b - 1)
                    g.tensor_tensor(a_rstd[i][:, :], a_veps[i][:, :], half_neg[:, 0:2 * J], ALU.pow
                                    ).then_inc(sa["a_rstd"], 1)

                def rstd_mid(b):
                    i, n = b % 2, b + 1
                    g.wait_ge(sa["c_mv"], n)
                    g.tensor_scalar(c_veps[i][:, :], c_mv[i][:, :, 1], EPS, None, ALU.add
                                    ).then_inc(sa["c_veps"], 1)
                    g.wait_ge(sa["c_veps"], n)
                    if b >= 2:
                        g.wait_ge(sa["h2"], b - 1)
                    g.tensor_tensor(c_rstd[i][:, :], c_veps[i][:, :], half_neg[:, 0:J], ALU.pow
                                    ).then_inc(sa["c_rstd"], 1)

                def differences(b):
                    i, n = b % 2, b + 1
                    g.wait_ge(sa["peak"], n)
                    if b >= 2:
                        g.wait_ge(sa["aa"], b - 1)
                    g.tensor_tensor(d_old[i][:, :], peak[i][:, 0:T], peak[i][:, 1:T + 1], ALU.subtract
                                    ).then_inc(sa["d_old"], 1)
                    g.wait_ge(sa["d_out"], n)
                    if b >= 2:
                        g.wait_ge(sa["num_new"], b - 1)
                    g.tensor_scalar(d_neg[i][:, :], d_out[i][:, :], 0.0, None, ALU.min
                                    ).then_inc(sa["d_neg"], 1)
                    g.wait_ge(sa["d_neg"], n)
                    g.tensor_tensor(d_pos[i][:, :], d_out[i][:, :], d_neg[i][:, :], ALU.subtract
                                    ).then_inc(sa["d_pos"], 1)

                def change(b):
                    i, n = b % 2, b + 1
                    g.wait_ge(sa["h2T"], n)
                    if b >= 2:
                        g.wait_ge(sa["mix_r"], b - 1)
                    g.tensor_tensor(dh[i][:, :], h2T[i][:, 1:T + 1], h2T[i][:, 0:T], ALU.subtract
                                    ).then_inc(sa["dh"], 1)

                def old_parts(b):
                    i, n = b % 2, b + 1
                    g.wait_ge(sa["e1"], n)
                    g.wait_ge(sa["aa"], n)
                    if b >= 2:
                        g.wait_ge(sa["num"], b - 1)
                    g.tensor_tensor(num_old[i][:, :], e1[i][:, :], aa[i][:, 0:T], ALU.mult
                                    ).then_inc(sa["num_old"], 1)
                    g.wait_ge(sa["bb"], n)
                    if b >= 2:
                        g.wait_ge(sa["wkv"], b - 1)
                    g.tensor_tensor(den_old[i][:, :], e1[i][:, :], bb[i][:, 0:T], ALU.mult
                                    ).then_inc(sa["den_old"], 1)
                    g.wait_ge(sa["den_old"], n)
                    g.wait_ge(sa["e2"], n)
                    g.tensor_tensor(den_old[i][:, :], den_old[i][:, :], e2[i][:, :], ALU.add
                                    ).then_inc(sa["den"], 1)

                def squares(b):
                    n = b + 1
                    for c in range(CC - KD, CC):
                        g.wait_ge(sa["pos_kk"], CC * b + c + 1)
                        g.tensor_tensor(kk[c][:, :], kk[c][:, :], kk[c][:, :], ALU.mult
                                        ).then_inc(sa["kk_g"], 1)

                def two_inputs(b):
                    i, n = b % 2, b + 1
                    g.wait_ge(sa["x2"], n)
                    g.tensor_tensor(flat(X, b), flat(X, b), x2[i][:, :, :].rearrange("p t d -> p (t d)"),
                                    ALU.add).then_inc(sa["x12"], 1)

                for b in range(NB + 1):
                    if b < NB:
                        rstd_in(b)
                    if b:
                        rstd_mid(b - 1)
                    if b < NB:
                        differences(b)
                    if b:
                        change(b - 1)
                        two_inputs(b - 1)
                        squares(b - 1)
                    if b < NB:
                        old_parts(b)

            for i in range(2):
                g.memset(h1T[i][:, 0:1], 0.0)
                g.memset(h2T[i][:, 0:1], 0.0)
                g.memset(aa[i][:, 0:1], 0.0)
                g.memset(bb[i][:, 0:1], 0.0)
                last = g.memset(peak[i][:, 0:1], LOWEST)
            last.then_inc(s_edge, 1)
            rsqrt_ffn(0)
            scatter(0)
            gather(0)
            rwkv()
            rsqrt_ffn(1)
            scatter(1)
            gather(1)

        @block.scalar
        def _(a):
            a.wait_ge(s_wtp, 1)
            a.copy(w_gateT[:, :, :].rearrange("p c f -> p (c f)"), bank[2][:, 0:FS])
            a.copy(w_upT[:, :, :].rearrange("p c f -> p (c f)"), bank[3][:, 0:FS])
            a.copy(w_downT[:, :, :].rearrange("p c d -> p (c d)"), bank[4][:, 0:SC * D])
            a.copy(w_routerT[:, :], bank[5][:, 0:E]).then_inc(s_wt, 1)

            def ffn_front(v):
                for b in range(NB):
                    a.wait_ge(s_xnTp, v * NB + b + 1)
                    a.copy(xnT[:, b, :], bank[b % 2][:, :]).then_inc(s_xnT, 1)
                a.wait_ge(s_best, v + 1)
                a.activation(th_score[:, :], best[:, :], ACT.Tanh, scale=0.5).then_inc(s_thsc, 1)
                for b in range(NB):
                    if b == 0:
                        a.wait_ge(s_score, v + 1)
                    if v:
                        a.wait_ge(s_x1, NB * v)
                    for t in range(J * b, J * b + J):
                        i = a.activation(xs[:, t, :], xn[:, t, :], ACT.Copy, scale=score[:, t:t + 1])
                    i.then_inc(s_xs, 1)
                for b in range(NB):
                    for c in range(SC):
                        n = (v * NB + b) * SC + c
                        a.wait_ge(s_sgu, n + 1)
                        if n >= SC:
                            a.wait_ge(s_sact, n + 1 - SC)
                        a.activation(sg[c][:, :], bank[2 + 2 * c][:, :], ACT.Silu).then_inc(s_ssilu, 1)

            def moe(v):
                def silu(i, k):
                    n = v * NBLK + i
                    a.wait_ge(s_mgu, n + 1)
                    if not isinstance(i, int) or n >= 2:
                        a.wait_ge(s_ma, n - 1)
                    a.activation(mg[k % 2][:, :], bank[2 + k % 2][:, 0:FM], ACT.Silu).then_inc(s_mg, 1)

                def turn(i, k):
                    n = v * NBLK + i
                    a.wait_ge(s_maTp, n + 1)
                    if not isinstance(i, int) or n >= 2:
                        a.wait_ge(s_my, n - 1)
                    a.copy(maT[k % 2][:, :, :].rearrange("p c f -> p (c f)"),
                           bank[4 + k % 2][:, 0:FM]).then_inc(s_maT, 1)

                def store(i, k):
                    a.wait_ge(s_yb, v * NBLK + i + 1)
                    a.dma_start(moe_dram[bass.ts(i, P), :], yb[k % NXB][:, :]
                                ).then_inc(s_yst[k % NXB], 16)

                o = v * NBLK
                LAG = 3
                for i in range(LAG + 1):
                    silu(i, o + i)
                    if i:
                        turn(i - 1, o + i - 1)
                store(0, o)
                first = LAG + 1
                loops = (NBLK - first) // NXB
                with a.Fori(0, loops) as r:
                    for k in range(NXB):
                        i = r * NXB + (first + k)
                        silu(i, o + first + k)
                        turn(i - 1, o + first + k - 1)
                        store(i - LAG, o + first + k - LAG)
                for i in range(first + loops * NXB, NBLK + LAG):
                    if i < NBLK:
                        silu(i, o + i)
                    if i <= NBLK:
                        turn(i - 1, o + i - 1)
                    store(i - LAG, o + i - LAG)

            def rwkv():
                def exp_row(b, name, out_, in_, scale=1.0, bias=0.0):
                    a.activation(out_[b % 2][:, :], in_[b % 2][:, :], ACT.Exp, scale=scale, bias=bias
                                 ).then_inc(sa[name], 1)

                def turned_in(b):
                    i, n = b % 2, b + 1
                    a.wait_ge(sa["h1Tp"], n)
                    if b == 0:
                        a.wait_ge(s_watt, 16 * (len(VEC) + 7))
                        a.wait_ge(s_edge, 1)
                    if b >= 2:
                        a.wait_ge(sa["r"], b - 1)
                    a.activation(h1T[i][:, 1:T + 1], bank[0][:, :], ACT.Identity,
                                 scale=vec["ln1_g"][:, 0:1], bias=vec["ln1_b"][:, 0:1]
                                 ).then_inc(sa["h1T"], 1)

                def turned_mid(b):
                    i, n = b % 2, b + 1
                    a.wait_ge(sa["h2Tp"], n)
                    if b >= 2:
                        a.wait_ge(sa["mix_r"], b - 1)
                    a.activation(h2T[i][:, 1:T + 1], bank[5][:, :], ACT.Identity,
                                 scale=vec["ln2_g"][:, 0:1], bias=vec["ln2_b"][:, 0:1]
                                 ).then_inc(sa["h2T"], 1)

                def state_exps(b):
                    n = b + 1
                    a.wait_ge(sa["d_now"], n)
                    if b >= 2:
                        a.wait_ge(sa["bb"], b - 1)
                    exp_row(b, "e2b", e2b, d_now)
                    a.wait_ge(sa["d_old"], n)
                    if b == 0:
                        a.wait_ge(s_prep, 1)
                    exp_row(b, "e1b", e1b, d_old, bias=decay[:, 0:1])

                def out_exps(b):
                    n = b + 1
                    a.wait_ge(sa["d_pos"], n)
                    if b >= 2:
                        a.wait_ge(sa["den"], b - 1)
                        a.wait_ge(sa["num_new"], b - 1)
                    exp_row(b, "e2", e2, d_neg)
                    exp_row(b, "e1", e1, d_pos, scale=-1.0)
                    a.wait_ge(sa["r"], n)
                    if b >= 2:
                        a.wait_ge(sa["rw"], b - 1)
                    a.activation(th_r[b % 2][:, :], bank[3][:, :], ACT.Tanh, scale=0.5
                                 ).then_inc(sa["th_r"], 1)

                def relus(b):
                    for c in range(CC):
                        a.wait_ge(sa["cwk"], CC * b + c + 1)
                        if b >= 1:
                            a.wait_ge(sa["cwv"], b)
                        a.activation(kk[c][:, :], bank[6 + c % 2][:, :], ACT.Relu
                                     ).then_inc(sa["pos_kk"], 1)

                def gate(b):
                    a.wait_ge(sa["rr"], b + 1)
                    if b >= 2:
                        a.wait_ge(sa["rcv"], b - 1)
                    a.activation(th_rr[b % 2][:, :], bank[4][:, :], ACT.Tanh, scale=0.5
                                 ).then_inc(sa["th_rr"], 1)

                for b in range(NB + 1):
                    if b < NB:
                        turned_in(b)
                    if b:
                        turned_mid(b - 1)
                    if b < NB:
                        state_exps(b)
                        out_exps(b)
                    if b:
                        relus(b - 1)
                        gate(b - 1)

            ffn_front(0)
            moe(0)
            a.wait_ge(s_watt, 16 * (len(VEC) + 7))
            a.activation(decay_exp[:, :], vec["time_decay"][:, :], ACT.Exp).then_inc(s_dexp, 1)
            rwkv()
            ffn_front(1)
            moe(1)

        @block.vector
        def _(d):
            def norm_ffn(v, b):
                n = v * NB + b + 1
                if v == 0:
                    d.wait_ge(s_x[b], 16)
                else:
                    d.wait_ge(sa["x_att"], b + 1)
                for t in range(J * b, J * b + J):
                    i = d.bn_stats(stats[:, t, :], X[:, t, :])
                i.then_inc(s_stats, 1)
                d.wait_ge(s_stats, n)
                for t in range(J * b, J * b + J):
                    i = d.bn_aggr(mv[:, t, :], stats[:, t, :])
                i.then_inc(s_mv, 1)

            def scale_ffn(v, b):
                d.wait_ge(s_rstd, v * NB + b + 1)
                for t in range(J * b, J * b + J):
                    i = d.tensor_scalar(xn[:, t, :], X[:, t, :], mv[:, t, 0:1], rstd[:, t:t + 1],
                                        ALU.subtract, ALU.mult)
                i.then_inc(s_xn, 1)

            def route(v):
                c = [v * 12]

                def done(ins):
                    c[0] += 1
                    ins.then_inc(s_rt, 1)
                    d.wait_ge(s_rt, c[0])

                logit = bank[7][:, 0:NT * E].rearrange("p (t e) -> p t e", e=E)
                d.wait_ge(s_logit, v * NB + NB)
                d.tensor_reduce(best[:, :], logit, AX.X, ALU.max).then_inc(s_best, 1)
                d.wait_ge(s_best, v + 1)
                done(d.tensor_tensor(is_best[:, :, :], logit,
                                     best[:, :].unsqueeze(2).to_broadcast([P, NT, E]), ALU.is_ge))
                done(d.tensor_tensor(ranked[:, :, :], is_best[:, :, :],
                                     rank[:, :].unsqueeze(1).to_broadcast([P, NT, E]), ALU.mult))
                done(d.tensor_reduce(top_rank[:, :], ranked[:, :, :], AX.X, ALU.max))
                d.tensor_tensor(onehot[:, :, :], rank[:, :].unsqueeze(1).to_broadcast([P, NT, E]),
                                top_rank[:, :].unsqueeze(2).to_broadcast([P, NT, E]),
                                ALU.is_equal).then_inc(s_onehot, 1)
                d.wait_ge(s_thsc, v + 1)
                d.tensor_scalar(score[:, :], th_score[:, :], 1.0, 0.5, ALU.add, ALU.mult
                                ).then_inc(s_score, 1)
                total = bank[6][:, 0:NT * E].rearrange("p (t e) -> p e t", e=E)
                d.wait_ge(s_count, v + 1)
                done(d.tensor_reduce(count[:, :], total, AX.X, ALU.add))
                done(d.tensor_scalar(blocks_f[:, :], count[:, :], (P - 1) / 2.0, 1.0 / P, ALU.add,
                                     ALU.mult))
                done(d.tensor_scalar(blocks[:, :], blocks_f[:, :], ROUND, -ROUND, ALU.add, ALU.add))
                done(d.tensor_tensor_scan(block_end[:, 1:E + 1], ones_row[:, :], blocks[:, :], 0.0,
                                          ALU.mult, ALU.add))
                d.tensor_copy(steps[:, :, 1:NT], total[:, :, 0:NT - 1])
                done(d.tensor_scalar(steps[:, :, 0], block_end[:, 0:E], float(P), None, ALU.mult))
                done(d.tensor_tensor_scan(tile_start[:, :, :].rearrange("p e t -> p (e t)"),
                                          carry[:, :, :].rearrange("p e t -> p (e t)"),
                                          steps[:, :, :].rearrange("p e t -> p (e t)"), 0.0,
                                          ALU.mult, ALU.add))
                done(d.tensor_tensor(slot_all[:, :, :],
                                     tile_start[:, :, :].rearrange("p e t -> p t e"),
                                     bank[5][:, 0:NT * E].rearrange("p (t e) -> p t e", e=E), ALU.add))
                done(d.tensor_tensor(slot_sel[:, :, :], slot_all[:, :, :], onehot[:, :, :], ALU.mult))
                done(d.tensor_reduce(slot_f[:, :], slot_sel[:, :, :], AX.X, ALU.add))
                d.tensor_copy(slot[:, :], slot_f[:, :]).then_inc(s_slot, 1)
                assert c[0] == 12 * (v + 1), c
                d.tensor_tensor(past[:, :, :],
                                block_no[:, :].unsqueeze(2).to_broadcast([1, NBLK, E - 1]),
                                block_end[0:1, 1:E].unsqueeze(1).to_broadcast([1, NBLK, E - 1]),
                                ALU.is_ge).then_inc(s_bexp, 1)
                d.wait_ge(s_bexp, 3 * v + 1)
                d.tensor_reduce(block_expert_f[:, :], past[:, :, :], AX.X, ALU.add).then_inc(s_bexp, 1)
                d.wait_ge(s_bexp, 3 * v + 2)
                d.tensor_copy(block_expert[:, :], block_expert_f[:, :]).then_inc(s_bexp, 1)

            def shared(v):
                def act_chunk(b, c):
                    n = (v * NB + b) * SC + c
                    d.wait_ge(s_ssilu, n + 1)
                    if n >= SC:
                        d.wait_ge(s_sdn, v * NB + b)
                    d.tensor_tensor(act[c][:, :], sg[c][:, :], bank[3 + 2 * c][:, :], ALU.mult
                                    ).then_inc(s_sact, 1)

                def residual(b):
                    d.wait_ge(s_sdn, v * NB + b + 1)
                    d.scalar_tensor_tensor(out=flat(X, b), in0=bank[6][:, :], scalar=0.5,
                                           in1=flat(X, b), op0=ALU.mult, op1=ALU.add
                                           ).then_inc(s_sres, 1)
                for b in range(NB):
                    act_chunk(b, 0)
                    if b:
                        residual(b - 1)
                    act_chunk(b, 1)
                residual(NB - 1)

            def moe(v):
                def xT(i, k):
                    n = v * NBLK + i
                    d.wait_ge(s_xbTp, n + 1)
                    if not isinstance(i, int) or n >= 2:
                        d.wait_ge(s_mgu, n - 1)
                    d.tensor_copy(xbT[k % 2][:, :], bank[k % 2][:, 0:P]
                                  ).then_inc(s_xbT, 1)

                def gate(i, k):
                    n = v * NBLK + i
                    d.wait_ge(s_mg, n + 1)
                    if not isinstance(i, int) or n >= 2:
                        d.wait_ge(s_maTp, n - 1)
                    d.tensor_tensor(ma[k % 2][:, :], mg[k % 2][:, :], bank[2 + k % 2][:, FM:2 * FM],
                                    ALU.mult).then_inc(s_ma, 1)

                def y(i, k):
                    n = v * NBLK + i
                    d.wait_ge(s_my, n + 1)
                    if n >= NXB:
                        d.wait_ge(s_yst[k % NXB], 16 * (n // NXB))
                    d.tensor_scalar(yb[k % NXB][:, :], bank[6 + k % 2][:, 0:P], 0.5,
                                    None, ALU.mult).then_inc(s_yb, 1)

                o = v * NBLK
                def slot(i):
                    if i + 2 < NBLK:
                        xT(i + 2, o + i + 2)
                    if 0 <= i < NBLK:
                        gate(i, o + i)
                    if i >= 2:
                        y(i - 2, o + i - 2)

                first = NXB + 2
                loops = (NBLK - 2 - first) // NXB
                for i in range(-2, first):
                    slot(i)
                with d.Fori(0, loops) as r:
                    for k in range(NXB):
                        i = r * NXB + (first + k)
                        n = o + first + k
                        xT(i + 2, n + 2)
                        gate(i, n)
                        d.wait_ge(s_my, i + (o - 1))
                        d.wait_ge(s_yst[(n - 2) % NXB], r * 16 + 16 * ((n - 2) // NXB))
                        d.tensor_scalar(yb[(n - 2) % NXB][:, :], bank[6 + n % 2][:, 0:P], 0.5,
                                        None, ALU.mult).then_inc(s_yb, 1)
                for i in range(first + loops * NXB, NBLK + 2):
                    slot(i)

            def ffn(v):
                for b in range(NB):
                    norm_ffn(v, b)
                    if b:
                        scale_ffn(v, b - 1)
                scale_ffn(v, NB - 1)
                route(v)
                shared(v)
                moe(v)

            def add_moe(v):
                for b in range(NB):
                    d.wait_ge(s_yg[b], 16 * J * (v + 1))
                    d.tensor_tensor(flat(X, b), flat(X, b), flat(yg, b), ALU.add).then_inc(s_x1, 1)

            def prepare():
                d.wait_ge(s_watt, 16 * (len(VEC) + 7))
                for j, m in enumerate(WMIX):
                    i = d.tensor_scalar(one_minus[:, j:j + 1], vec["tm_mix_" + m][:, :], -1.0, 1.0,
                                        ALU.mult, ALU.add)
                i.then_inc(s_omix, 1)
                d.wait_ge(s_omix, 1)
                for j, m in enumerate(WMIX):
                    d.tensor_scalar(w_now[m][:, :], w_tm[m][:, :], vec["tm_mix_" + m][:, 0:1], None, ALU.mult)
                    i = d.tensor_scalar(w_prev[m][:, :], w_tm[m][:, :], one_minus[:, j:j + 1], None, ALU.mult)
                i.then_inc(s_wmix, 1)

            def prepare_decay():
                d.wait_ge(s_dexp, 1)
                d.tensor_scalar(decay[:, :], decay_exp[:, :], -1.0, None, ALU.mult).then_inc(s_prep, 1)
                d.wait_ge(s_prep, 1)
                d.tensor_copy(decay_row[:, :], decay[:, 0:1].to_broadcast([P, T])).then_inc(s_prep, 1)
                d.wait_ge(s_prep, 2)

            def rwkv():
                def wait(name, n):
                    if n > 0:
                        d.wait_ge(sa[name], n)

                def inputs(b):
                    i, n = b % 2, b + 1
                    d.wait_ge(s_yg[b], 16 * J)
                    d.tensor_tensor(flat(X, b), flat(X, b), flat(yg, b), ALU.add).then_inc(s_x1, 1)
                    d.wait_ge(s_x1, n)
                    for j in range(J):
                        m = d.bn_stats(a_stats[i][:, j, :], X[:, J * b + j, :])
                    m.then_inc(sa["a_stats"], 1)
                    d.wait_ge(sa["a_stats"], n)
                    wait("a_veps", b - 1)
                    for j in range(J):
                        m = d.bn_aggr(a_mv[i][:, j, :], a_stats[i][:, j, :])
                    m.then_inc(sa["a_mv"], 1)

                def mid(b):
                    i, n = b % 2, b + 1
                    d.wait_ge(sa["wo"], n)
                    wait("x12", b - 1)
                    d.scalar_tensor_tensor(out=x2[i][:, :, :].rearrange("p t d -> p (t d)"),
                                           in0=bank[4][:, :], scalar=0.5,
                                           in1=a_in[i][:, :, :].rearrange("p t d -> p (t d)"),
                                           op0=ALU.mult, op1=ALU.add).then_inc(sa["x2"], 1)
                    d.wait_ge(sa["x2"], n)
                    for j in range(J):
                        m = d.bn_stats(c_stats[i][:, j, :], x2[i][:, j, :])
                    m.then_inc(sa["c_stats"], 1)
                    d.wait_ge(sa["c_stats"], n)
                    wait("c_veps", b - 1)
                    for j in range(J):
                        m = d.bn_aggr(c_mv[i][:, j, :], c_stats[i][:, j, :])
                    m.then_inc(sa["c_mv"], 1)

                def norm_in(b):
                    i, n = b % 2, b + 1
                    d.wait_ge(sa["a_rstd"], n)
                    wait("h1Tp", b - 1)
                    for j in range(J):
                        d.tensor_scalar(h1[i][:, j, :], X[:, J * b + j, :], a_mv[i][:, j, 0:1],
                                        a_rstd[i][:, J + j:J + j + 1], ALU.subtract, ALU.mult)
                        m = d.tensor_scalar(a_in[i][:, j, :], X[:, J * b + j, :], a_mv[i][:, j, 0:1],
                                            a_rstd[i][:, j:j + 1], ALU.subtract, ALU.mult)
                    m.then_inc(sa["a_norm"], 1)

                def norm_mid(b):
                    i, n = b % 2, b + 1
                    d.wait_ge(sa["c_rstd"], n)
                    wait("h2Tp", b - 1)
                    for j in range(J):
                        m = d.tensor_scalar(h2[i][:, j, :], x2[i][:, j, :], c_mv[i][:, j, 0:1],
                                            c_rstd[i][:, j:j + 1], ALU.subtract, ALU.mult)
                    m.then_inc(sa["h2"], 1)

                def peaks(b):
                    i, n = b % 2, b + 1
                    d.wait_ge(sa["k"], n)
                    if b == 0:
                        prepare_decay()
                        d.wait_ge(s_edge, 1)
                    wait("d_old", b - 1)
                    d.tensor_tensor_scan(peak[i][:, 1:T + 1], decay_row[:, :], bank[1][:, :], LOWEST,
                                         ALU.add, ALU.max).then_inc(sa["peak"], 1)
                    d.wait_ge(sa["peak"], n)
                    d.tensor_tensor(d_now[i][:, :], bank[1][:, :], peak[i][:, 1:T + 1], ALU.subtract
                                    ).then_inc(sa["d_now"], 1)
                    wait("den_old", b - 1)
                    d.scalar_tensor_tensor(out=d_out[i][:, :], in0=bank[1][:, :],
                                           scalar=vec["time_first"][:, 0:1], in1=peak[i][:, 0:T],
                                           op0=ALU.add, op1=ALU.subtract).then_inc(sa["d_out"], 1)

                def mixes(b):
                    i, n = b % 2, b + 1
                    d.wait_ge(sa["dh"], n)
                    wait("cwk", CC * (b - 1))
                    d.scalar_tensor_tensor(out=mix_k[i][:, :], in0=dh[i][:, :],
                                           scalar=vec["cm_mix_k"][:, 0:1], in1=h2T[i][:, 0:T],
                                           op0=ALU.mult, op1=ALU.add).then_inc(sa["mix_k"], 1)
                    wait("rr", b - 1)
                    d.scalar_tensor_tensor(out=mix_r[i][:, :], in0=dh[i][:, :],
                                           scalar=vec["cm_mix_r"][:, 0:1], in1=h2T[i][:, 0:T],
                                           op0=ALU.mult, op1=ALU.add).then_inc(sa["mix_r"], 1)

                def states(b):
                    i, n = b % 2, b + 1
                    d.wait_ge(sa["e2b"], n)
                    d.wait_ge(sa["v"], n)
                    d.tensor_tensor(kv[i][:, :], e2b[i][:, :], bank[2][:, :], ALU.mult
                                    ).then_inc(sa["kv"], 1)
                    d.wait_ge(sa["e1b"], n)
                    wait("den", b - 1)
                    d.tensor_tensor_scan(bb[i][:, 1:T + 1], e1b[i][:, :], e2b[i][:, :], 0.0,
                                         ALU.mult, ALU.add).then_inc(sa["bb"], 1)
                    d.wait_ge(sa["kv"], n)
                    wait("num_old", b - 1)
                    d.tensor_tensor_scan(aa[i][:, 1:T + 1], e1b[i][:, :], kv[i][:, :], 0.0,
                                         ALU.mult, ALU.add).then_inc(sa["aa"], 1)
                    d.wait_ge(sa["e2"], n)
                    wait("wo", b - 1)
                    d.tensor_tensor(num_new[i][:, :], e2[i][:, :], bank[2][:, :], ALU.mult
                                    ).then_inc(sa["num_new"], 1)

                def squares(b):
                    for c in range(KD):
                        d.wait_ge(sa["pos_kk"], CC * b + c + 1)
                        d.tensor_tensor(kk[c][:, :], kk[c][:, :], kk[c][:, :], ALU.mult
                                        ).then_inc(sa["kk_d"], 1)

                def divide(b):
                    i, n = b % 2, b + 1
                    d.wait_ge(sa["num_old"], n)
                    d.wait_ge(sa["num_new"], n)
                    d.tensor_tensor(num_new[i][:, :], num_new[i][:, :], num_old[i][:, :], ALU.add
                                    ).then_inc(sa["num"], 1)
                    d.wait_ge(sa["den"], n)
                    d.reciprocal(den_old[i][:, :], den_old[i][:, :]).then_inc(sa["rden"], 1)
                    d.wait_ge(sa["rden"], n)
                    d.tensor_tensor(num_new[i][:, :], num_new[i][:, :], den_old[i][:, :], ALU.mult
                                    ).then_inc(sa["wkv"], 1)
                    d.wait_ge(sa["wkv"], n)
                    d.wait_ge(sa["th_r"], n)
                    d.scalar_tensor_tensor(out=rw[i][:, :], in0=th_r[i][:, :], scalar=1.0,
                                           in1=num_new[i][:, :], op0=ALU.add, op1=ALU.mult
                                           ).then_inc(sa["rw"], 1)

                def outputs(b):
                    i, n = b % 2, b + 1
                    d.wait_ge(sa["th_rr"], n)
                    d.wait_ge(sa["cwv"], n)
                    d.scalar_tensor_tensor(out=th_rr[i][:, :], in0=th_rr[i][:, :], scalar=1.0,
                                           in1=bank[5][:, :], op0=ALU.add, op1=ALU.mult
                                           ).then_inc(sa["rcv"], 1)
                    d.wait_ge(sa["rcv"], n)
                    d.wait_ge(sa["x12"], n)
                    d.scalar_tensor_tensor(out=flat(X, b), in0=th_rr[i][:, :], scalar=0.5,
                                           in1=flat(X, b), op0=ALU.mult, op1=ALU.add
                                           ).then_inc(sa["x_att"], 1)

                for b in range(NB + 1):
                    if b < NB:
                        inputs(b)
                    if b:
                        mid(b - 1)
                    if b < NB:
                        norm_in(b)
                    if b:
                        norm_mid(b - 1)
                    if b < NB:
                        peaks(b)
                    if b:
                        mixes(b - 1)
                    if b < NB:
                        states(b)
                    if b:
                        squares(b - 1)
                    if b < NB:
                        divide(b)
                    if b:
                        outputs(b - 1)

            ffn(0)
            prepare()
            rwkv()
            ffn(1)
            add_moe(1)

        @block.tensor
        def _(t):
            t.wait_ge(s_const, 9)
            t.wait_ge(s_wsh, 64)
            for c in range(SC):
                t.transpose(bank[2][:, c * P:c * P + P], w_gate_raw[:, c, :], ident[:, :])
                t.transpose(bank[3][:, c * P:c * P + P], w_up_raw[:, c, :], ident[:, :])
                t.transpose(bank[4][:, c * P:c * P + P], w_down_raw[:, c * P:c * P + P], ident[:, :])
            t.transpose(bank[5][:, 0:E], w_router_raw[:, :], ident[0:E, 0:E]).then_inc(s_wtp, 1)

            def front(v):
                def turn(b):
                    t.wait_ge(s_xn, v * NB + b + 1)
                    if v * NB + b >= 2:
                        t.wait_ge(s_xnT, v * NB + b - 1)
                    for j in range(J):
                        m = t.transpose(bank[b % 2][:, j * P:j * P + P], xn[:, J * b + j, :], ident[:, :])
                    m.then_inc(s_xnTp, 1)

                def router(b):
                    t.wait_ge(s_xnT, v * NB + b + 1)
                    if v == 0 and b == 0:
                        t.wait_ge(s_wt, 1)
                    for j in range(J):
                        k = J * b + j
                        m = t.matmul(bank[7][:, k * E:k * E + E], xnT[:, b, j * P:j * P + P],
                                     w_routerT[:, :], start=True, stop=True)
                    m.then_inc(s_logit, 1)

                if v:
                    t.wait_ge(s_xbT, v * NBLK)
                for b in range(NB):
                    turn(b)
                    if b:
                        router(b - 1)
                router(NB - 1)

            def count_tokens(v):
                t.wait_ge(s_onehot, v + 1)
                oh = onehot[:, :, :].rearrange("p t e -> p (t e)")
                t.matmul(bank[6][:, 0:NT * E], ones[:, :], oh, start=True, stop=True)
                t.matmul(bank[5][:, 0:NT * E], before[:, :], oh, start=True, stop=True
                         ).then_inc(s_count, 1)

            def shared(v):
                def gate_up_chunk(b, c):
                    n = (v * NB + b) * SC + c
                    if n >= SC:
                        t.wait_ge(s_sact, n + 1 - SC)
                    t.matmul(bank[2 + 2 * c][:, :], w_gateT[:, c, :], xnT[:, b, :], start=True, stop=True)
                    t.matmul(bank[3 + 2 * c][:, :], w_upT[:, c, :], xnT[:, b, :], start=True, stop=True
                             ).then_inc(s_sgu, 1)

                def down_tiles(b):
                    t.wait_ge(s_sact, (v * NB + b + 1) * SC)
                    if v * NB + b:
                        t.wait_ge(s_sres, v * NB + b)
                    for j in range(J):
                        for c in range(SC):
                            m = t.matmul(bank[6][:, j * P:j * P + P], act[c][:, j * P:j * P + P],
                                         w_downT[:, c, :], start=(c == 0), stop=(c == SC - 1))
                    m.then_inc(s_sdn, 1)

                for b in range(NB):
                    gate_up_chunk(b, 0)
                    if b == 0:
                        count_tokens(v)
                        t.wait_ge(s_slot, v + 1)
                    gate_up_chunk(b, 1)
                    if b:
                        down_tiles(b - 1)
                down_tiles(NB - 1)

            def moe(v):
                def turn_x(i, k):
                    n = v * NBLK + i
                    kb = k % NXB
                    t.wait_ge(s_xb[kb], 16 * (n // NXB + 1))
                    if n >= 2:
                        t.wait_ge(s_xbT, n - 1)
                    t.transpose(bank[k % 2][:, 0:P], xb[kb][:, :], ident[:, :]
                                ).then_inc(s_xbTp, 1)

                def gate_up_block(i, k, e):
                    n = v * NBLK + i
                    t.wait_ge(s_xbT, n + 1)
                    if not isinstance(i, int) or n >= 2:
                        t.wait_ge(s_ma, n - 1)
                    t.matmul(bank[2 + k % 2][:, :], xbT[k % 2][:, :], gate_up[:, e, :],
                             start=True, stop=True).then_inc(s_mgu, 1)

                def turn_a(i, k):
                    n = v * NBLK + i
                    t.wait_ge(s_ma, n + 1)
                    if not isinstance(i, int) or n >= 2:
                        t.wait_ge(s_maT, n - 1)
                    for c in range(FC):
                        m = t.transpose(bank[4 + k % 2][:, c * P:c * P + P], ma[k % 2][:, c * P:c * P + P], ident[:, :])
                    m.then_inc(s_maTp, 1)

                def down_block(i, k, e):
                    n = v * NBLK + i
                    t.wait_ge(s_maT, n + 1)
                    if not isinstance(i, int) or n >= 2:
                        t.wait_ge(s_yb, n - 1)
                    for c in range(FC):
                        m = t.matmul(bank[6 + k % 2][:, 0:P], maT[k % 2][:, c, :],
                                     down[:, e, c, :], start=(c == 0), stop=(c == FC - 1))
                    m.then_inc(s_my, 1)

                def expert(i):
                    return t.value_load(block_expert[0:1, bass.ds(i, 1)], min_val=0, max_val=E - 1)

                t.wait_ge(s_bexp, 3 * v + 3)
                t.wait_ge(s_sres, (v + 1) * NB)
                if v == 0:
                    t.wait_ge(s_wmoe, 16 * 2 * (E // 4))
                o = v * NBLK

                def slot_static(i):
                    if 0 <= i + 2 < NBLK:
                        turn_x(i + 2, o + i + 2)
                    if 0 <= i + 1 < NBLK:
                        gate_up_block(i + 1, o + i + 1, expert(i + 1))
                    if 0 <= i < NBLK:
                        turn_a(i, o + i)
                    if 0 <= i - 1 < NBLK:
                        down_block(i - 1, o + i - 1, expert(i - 1))

                FIRST = 3
                full = (NBLK - 2 - FIRST) // NXB * NXB
                for i in range(-2, FIRST):
                    slot_static(i)
                with t.Fori(0, full // NXB) as r:
                    for k in range(NXB):
                        i = r * NXB + (FIRST + k)
                        ahead = o + FIRST + k + 2
                        t.wait_ge(s_xb[ahead % NXB], r * 16 + 16 * (ahead // NXB + 1))
                        t.wait_ge(s_xbT, i + (o + 1))
                        t.transpose(bank[ahead % 2][:, 0:P],
                                    xb[ahead % NXB][:, :], ident[:, :]).then_inc(s_xbTp, 1)
                        gate_up_block(i + 1, ahead - 1, expert(i + 1))
                        turn_a(i, ahead - 2)
                        down_block(i - 1, ahead - 3, expert(i - 1))
                for i in range(FIRST + full, NBLK + 1):
                    slot_static(i)

            def ffn(v):
                front(v)
                shared(v)
                moe(v)

            def rwkv():
                def wait(name, n):
                    if n > 0:
                        t.wait_ge(sa[name], n)

                def turn(b, bank_, src, name):
                    for j in range(J):
                        m = t.transpose(bank_[:, j * P:j * P + P], src[b % 2][:, j, :], ident[:, :])
                    m.then_inc(sa[name], 1)

                def turn_in(b):
                    t.wait_ge(sa["a_norm"], b + 1)
                    wait("h1T", b)
                    turn(b, bank[0], h1, "h1Tp")

                def turn_mid(b):
                    t.wait_ge(sa["h2"], b + 1)
                    wait("rcv", b)
                    turn(b, bank[5], h2, "h2Tp")

                def kvr(b):
                    i = b % 2
                    t.wait_ge(sa["h1T"], b + 1)
                    if b == 0:
                        t.wait_ge(s_wmix, 1)
                        t.wait_ge(s_yb, NBLK)
                    for m, bk, free in (("k", 1, "d_out"), ("v", 2, "num_new"), ("r", 3, "th_r")):
                        wait(free, b)
                        t.matmul(bank[bk][:, :], w_now[m][:, :], h1T[i][:, 1:T + 1], start=True, stop=False)
                        t.matmul(bank[bk][:, :], w_prev[m][:, :], h1T[i][:, 0:T], start=False, stop=True
                                 ).then_inc(sa[m], 1)

                def channel(b):
                    i = b % 2
                    t.wait_ge(sa["mix_k"], b + 1)
                    for c in range(CC):
                        wait("pos_kk", CC * b + c - 1)
                        t.matmul(bank[6 + c % 2][:, :], cwk[:, c * P:c * P + P], mix_k[i][:, :],
                                 start=True, stop=True).then_inc(sa["cwk"], 1)
                    t.wait_ge(sa["mix_r"], b + 1)
                    t.wait_ge(sa["x2"], b + 1)
                    for j in range(J):
                        m = t.matmul(bank[4][:, j * P:j * P + P], mix_r[i][:, j * P:j * P + P], cwr[:, :],
                                     start=True, stop=True)
                    m.then_inc(sa["rr"], 1)
                    t.wait_ge(sa["kk_d"], KD * (b + 1))
                    t.wait_ge(sa["kk_g"], (CC - KD) * (b + 1))
                    t.wait_ge(sa["h2T"], b + 1)
                    for j in range(J):
                        for c in range(CC):
                            m = t.matmul(bank[5][:, j * P:j * P + P], kk[c][:, j * P:j * P + P],
                                         cwv[:, c, :], start=(c == 0), stop=(c == CC - 1))
                    m.then_inc(sa["cwv"], 1)

                def project(b):
                    t.wait_ge(sa["rw"], b + 1)
                    wait("th_rr", b)
                    for j in range(J):
                        m = t.matmul(bank[4][:, j * P:j * P + P], rw[b % 2][:, j * P:j * P + P], wo[:, :],
                                     start=True, stop=True)
                    m.then_inc(sa["wo"], 1)

                for b in range(NB + 1):
                    if b < NB:
                        turn_in(b)
                    if b:
                        turn_mid(b - 1)
                    if b < NB:
                        kvr(b)
                    if b:
                        channel(b - 1)
                    if b < NB:
                        project(b)

            ffn(0)
            rwkv()
            ffn(1)


_INS = ["L0_attn_x", "L0_attn_ln1_g", "L0_attn_ln1_b", "L0_attn_ln2_g", "L0_attn_ln2_b",
        "L0_attn_tm_mix_k", "L0_attn_tm_mix_v", "L0_attn_tm_mix_r", "L0_attn_time_decay",
        "L0_attn_time_first", "L0_attn_wk", "L0_attn_wv", "L0_attn_wr", "L0_attn_wo",
        "L0_attn_cm_mix_k", "L0_attn_cm_mix_r", "L0_attn_cwk", "L0_attn_cwv", "L0_attn_cwr",
        "L0_ffn_w_router", "L0_ffn_gate_up_proj", "L0_ffn_down_proj", "L0_ffn_w_gate",
        "L0_ffn_w_up", "L0_ffn_w_down"]


def kernel(**inputs):
    import numpy as _np
    import concourse.bacc as _bacc
    from concourse import mybir as _mybir
    from concourse.bass_utils import run_bass_kernel_spmd as _run

    nc = _bacc.Bacc("TRN2", target_bir_lowering=False, num_devices=1)
    arrays, args = {}, {}
    for name in _INS:
        a = _np.ascontiguousarray(inputs[name])
        arrays[f"in_{name}_dram"] = a
        args[name] = nc.dram_tensor(f"in_{name}_dram", a.shape, _mybir.dt.from_np(a.dtype),
                                    kind="ExternalInput").ap()
    shape = inputs["L0_attn_x"].shape
    out = nc.dram_tensor("out_0_dram", shape, _mybir.dt.float32, kind="ExternalOutput").ap()
    macaron_kernel(nc, args, out)
    r = _run(nc, [arrays], core_ids=[0])
    return r.results[0]["out_0_dram"]
```

```python
from contextlib import ExitStack

import concourse.bass as bass
from concourse import mybir

ALU = mybir.AluOpType
ACT = mybir.ActivationFunctionType
AX = mybir.AxisListType
F32 = mybir.dt.float32
BF16 = mybir.dt.bfloat16
I32 = mybir.dt.int32

P = 128
EPS = 1e-5
ROUND = float(2 ** 23)
LOWEST = -1e38


def macaron_kernel(nc, t_in, out):
    x_in = t_in["L0_attn_x"]
    NB, T, D = x_in.shape
    assert D == P and T % P == 0
    J = T // P
    NT = NB * J
    E, _, F2 = t_in["L0_ffn_gate_up_proj"].shape
    FM = F2 // 2
    FC = FM // P
    FS = t_in["L0_ffn_w_gate"].shape[0]
    SC = FS // P
    CF = t_in["L0_attn_cwk"].shape[1]
    CC = CF // P
    NBLK = NT + E - 1
    WMIX = ("k", "v", "r")

    ctx = ExitStack()
    with ctx:
        def sb(name, shape, dt=F32):
            return ctx.enter_context(nc.sbuf_tensor(name, shape, dt))

        def sem(name):
            return ctx.enter_context(nc.semaphore(name))

        bank = [ctx.enter_context(nc.psum_tensor(f"bank{i}", [P, 512], F32)) for i in range(8)]

        slots_dram = nc.dram_tensor("slots_dram", [NBLK * P, D], F32, kind="Internal").ap()
        moe_dram = nc.dram_tensor("moe_dram", [NBLK * P, D], F32, kind="Internal").ap()

        ROW = F2 + FC * D
        experts = sb("experts", [P, E * ROW])
        experts_e = experts[:, :].rearrange("p (e w) -> p e w", e=E)
        w_gate_raw = sb("w_gate_raw", [P, SC, D])
        w_up_raw = sb("w_up_raw", [P, SC, D])
        w_down_raw = sb("w_down_raw", [P, FS])
        w_router_raw = sb("w_router_raw", [E, D])
        w_gateT = sb("w_gateT", [P, SC, P])
        w_upT = sb("w_upT", [P, SC, P])
        w_downT = sb("w_downT", [P, SC, D])
        w_routerT = sb("w_routerT", [P, E])
        w_tm = {m: sb(f"w{m}", [P, D]) for m in WMIX}
        w_now = {m: sb(f"w{m}_now", [P, D]) for m in WMIX}
        w_prev = {m: sb(f"w{m}_prev", [P, D]) for m in WMIX}
        wo = sb("wo", [P, D])
        cwk = sb("cwk", [P, CF])
        cwr = sb("cwr", [P, D])
        cwv = sb("cwv", [P, CC, D])
        VEC = ["ln1_g", "ln1_b", "ln2_g", "ln2_b", "tm_mix_k", "tm_mix_v", "tm_mix_r",
               "time_decay", "time_first", "cm_mix_k", "cm_mix_r"]
        vec = {v: sb(v, [P, 1]) for v in VEC}
        one_minus = sb("one_minus", [P, 3])
        decay_exp = sb("decay_exp", [P, 1])
        decay = sb("decay", [P, 1])
        decay_row = sb("decay_row", [P, T])
        ident = sb("ident", [P, P])
        before = sb("before", [P, P], BF16)
        ones = sb("ones", [P, P], BF16)
        rank = sb("rank", [P, E])
        carry = sb("carry", [P, E, NT])
        block_no = sb("block_no", [1, NBLK])
        half_neg = sb("half_neg", [P, 2 * NT])
        ones_row = sb("ones_row", [P, E])
        zero_rows = sb("zero_rows", [P, 8 * D])

        X = sb("X", [P, NT, D])
        xn = sb("xn", [P, NT, D])
        xs = sb("xs", [P, NT, D])
        xnT = sb("xnT", [P, NB, T])
        yg = xs
        stats = sb("stats", [P, NT, 6])
        mv = sb("mv", [P, NT, 2])
        veps = sb("veps", [P, 2 * NT])
        rstd = sb("rstd", [P, 2 * NT])
        best = sb("best", [P, NT])
        th_score = sb("th_score", [P, NT])
        score = sb("score", [P, NT])
        is_best = sb("is_best", [P, NT, E])
        ranked = sb("ranked", [P, NT, E])
        top_rank = sb("top_rank", [P, NT])
        onehot = sb("onehot", [P, NT, E], BF16)
        count = sb("count", [P, E])
        blocks_f = sb("blocks_f", [P, E])
        blocks = sb("blocks", [P, E])
        block_end = sb("block_end", [P, E + 1])
        steps = sb("steps", [P, E, NT])
        tile_start = sb("tile_start", [P, E, NT])
        slot_all = sb("slot_all", [P, NT, E])
        slot_sel = sb("slot_sel", [P, NT, E])
        slot_f = sb("slot_f", [P, NT])
        slot = sb("slot", [P, NT], I32)
        past = sb("past", [1, NBLK, E - 1])
        block_expert_f = sb("block_expert_f", [1, NBLK])
        block_row = sb("block_row", [1, NBLK], I32)
        sg = [sb(f"sg{c}", [P, T]) for c in range(SC)]
        act = [sb(f"act{c}", [P, T]) for c in range(SC)]
        NXB = 4
        xb = [sb(f"xb{i}", [P, D]) for i in range(NXB)]
        xbT = [sb(f"xbT{i}", [P, P]) for i in range(2)]
        mg = [sb(f"mg{i}", [P, FM]) for i in range(2)]
        ma = [sb(f"ma{i}", [P, FM]) for i in range(2)]
        maT = [sb(f"maT{i}", [P, FC, P]) for i in range(2)]
        yb = [sb(f"yb{i}", [P, D]) for i in range(NXB)]

        def tiles(ap, b):
            return ap[:, J * b:J * b + J, :]

        def flat(ap, b):
            return ap[:, J * b:J * b + J, :].rearrange("p t d -> p (t d)")

        def two(name, shape):
            return [sb(f"{name}{i}", shape) for i in range(2)]

        a_stats = two("a_stats", [P, J, 6])
        a_mv = two("a_mv", [P, J, 2])
        a_veps = two("a_veps", [P, 2 * J])
        a_rstd = two("a_rstd", [P, 2 * J])
        h1 = [tiles(xn, i) for i in range(2)]
        a_in = [tiles(xn, 2 + i) for i in range(2)]
        x2 = [xnT[:, i, :].rearrange("p (t d) -> p t d", d=D) for i in range(2)]
        h2 = [xnT[:, 2 + i, :].rearrange("p (t d) -> p t d", d=D) for i in range(2)]
        dh = sg
        kk = [zero_rows[:, 0:T], zero_rows[:, T:2 * T], act[0], act[1]]
        h1T = two("h1T", [P, T + 1])
        peak = two("peak", [P, T + 1])
        d_now = two("d_now", [P, T])
        d_old = two("d_old", [P, T])
        d_out = two("d_out", [P, T])
        d_neg = two("d_neg", [P, T])
        d_pos = d_out
        e2b, e1b, e2, e1 = d_now, d_old, d_neg, d_pos
        kv = two("kv", [P, T])
        aa = two("aa", [P, T + 1])
        bb = two("bb", [P, T + 1])
        num_new = two("num_new", [P, T])
        num_old = two("num_old", [P, T])
        den_old = two("den_old", [P, T])
        th_r = two("th_r", [P, T])
        rw = num_new
        c_stats = two("c_stats", [P, J, 6])
        c_mv = two("c_mv", [P, J, 2])
        c_veps = two("c_veps", [P, J])
        c_rstd = two("c_rstd", [P, J])
        h2T = two("h2T", [P, T + 1])
        mix_k = two("mix_k", [P, T])
        mix_r = two("mix_r", [P, T])
        th_rr = two("th_rr", [P, T])

        s_x = [sem(f"s_xin{b}") for b in range(NB)]
        s_wsh = sem("s_wsh")
        s_wmoe = sem("s_wmoe")
        s_watt = sem("s_watt")
        s_zero_set = sem("s_zero_set")
        s_zeroed = sem("s_zeroed")
        s_cmem = sem("s_cmem")
        s_const = sem("s_const")
        s_wtp = sem("s_wtp")
        s_wt = sem("s_wt")
        s_stats = sem("s_stats")
        s_mv = sem("s_mv")
        s_veps = sem("s_veps")
        s_rstd = sem("s_rstd")
        s_xn = sem("s_xn")
        s_xnTp = sem("s_xnTp")
        s_xnT = sem("s_xnT")
        s_logit = sem("s_logit")
        s_best = sem("s_best")
        s_thsc = sem("s_thsc")
        s_score = sem("s_score")
        s_xs = sem("s_xs")
        s_rt = sem("s_rt")
        s_onehot = sem("s_onehot")
        s_count = sem("s_count")
        s_slot = sem("s_slot")
        s_bexp = sem("s_bexp")
        s_scat = sem("s_scat")
        s_sgu = sem("s_sgu")
        s_ssilu = sem("s_ssilu")
        s_sact = sem("s_sact")
        s_sdn = sem("s_sdn")
        s_sres = sem("s_sres")
        s_xb = [sem(f"s_xb{i}") for i in range(NXB)]
        s_xbTp = sem("s_xbTp")
        s_xbT = sem("s_xbT")
        s_mgu = sem("s_mgu")
        s_mg = sem("s_mg")
        s_ma = sem("s_ma")
        s_maTp = sem("s_maTp")
        s_maT = sem("s_maT")
        s_my = sem("s_my")
        s_yb = sem("s_yb")
        s_yst = [sem(f"s_yst{i}") for i in range(NXB)]
        s_yg = [sem(f"s_yg{b}") for b in range(NB)]
        s_x1 = sem("s_x1")
        s_out = sem("s_out")
        def pipelined(steps):
            for j in range(NB + max(lag for _, lag in steps)):
                for step, lag in steps:
                    if 0 <= j - lag < NB:
                        step(j - lag)

        ATT = ["a_stats", "a_mv", "a_veps", "a_rstd", "a_norm", "h1Tp", "h1T", "k", "v", "r", "th_r", "peak",
               "d_now", "d_out", "d_old", "d_neg", "d_pos", "e2b", "e1b", "e2", "e1", "kv", "aa", "bb",
               "num_new", "num_old", "den_old", "den", "num", "rden", "wkv", "rw", "wo", "x2", "c_stats",
               "c_mv", "c_veps", "c_rstd", "h2", "h2Tp", "h2T", "dh", "mix_k", "mix_r", "cwk", "pos_kk",
               "kk", "a_in", "rr", "th_rr", "cwv", "x12", "rcv", "x_att"]
        sa = {n: sem("s_" + n + "_a") for n in ATT}
        s_edge = sem("s_edge")
        s_omix = sem("s_omix")
        s_wmix = sem("s_wmix")
        s_dexp = sem("s_dexp")
        s_prep = sem("s_prep")

        x_dram = x_in.rearrange("b (t p) d -> b p t d", p=P)
        out_dram = out.rearrange("b (t p) d -> b p t d", p=P)

        block = ctx.enter_context(nc.Block())

        @block.sync
        def _(sp):
            for b in range(NB):
                sp.dma_start(tiles(X, b), x_dram[b]).then_inc(s_x[b], 16)
                if b == 0:
                    sp.dma_start(w_router_raw[:, :], t_in["L0_ffn_w_router"]).then_inc(s_wsh, 16)
                    sp.dma_start(w_gate_raw[:, :, :], t_in["L0_ffn_w_gate"].rearrange(
                        "(c p) d -> p c d", p=P)).then_inc(s_wsh, 16)
                    sp.dma_start(w_up_raw[:, :, :], t_in["L0_ffn_w_up"].rearrange(
                        "(c p) d -> p c d", p=P)).then_inc(s_wsh, 16)
                    sp.dma_start(w_down_raw[:, :], t_in["L0_ffn_w_down"]).then_inc(s_wsh, 16)
            sp.wait_ge(s_zero_set, 1)
            q = 0
            while q < NBLK * P:
                n = min(8 * P, NBLK * P - q)
                sp.dma_start(slots_dram[q:q + n, :].rearrange("(p r) d -> p (r d)", p=P),
                             zero_rows[:, :n // P * D]).then_inc(s_zeroed, 16)
                q += n
            for e in range(0, E, 4):
                sp.dma_start(experts_e[:, e:e + 4, 0:F2], t_in["L0_ffn_gate_up_proj"][e:e + 4].rearrange(
                    "e h f -> h e f")).then_inc(s_wmoe, 16)
                for i in range(e, e + 4):
                    sp.dma_start(experts_e[:, i, F2:ROW].rearrange("p (c d) -> p c d", c=FC),
                                 t_in["L0_ffn_down_proj"][i].rearrange("(c p) d -> p c d", p=P)
                                 ).then_inc(s_wmoe, 16)
            for v in VEC:
                sp.dma_start(vec[v][:, :], t_in["L0_attn_" + v].rearrange("(p a) -> p a", a=1)
                             ).then_inc(s_watt, 16)
            for m in WMIX:
                sp.dma_start(w_tm[m][:, :], t_in["L0_attn_w" + m]).then_inc(s_watt, 16)
            sp.dma_start(wo[:, :], t_in["L0_attn_wo"]).then_inc(s_watt, 16)
            sp.dma_start(cwk[:, :], t_in["L0_attn_cwk"]).then_inc(s_watt, 16)
            sp.dma_start(cwr[:, :], t_in["L0_attn_cwr"]).then_inc(s_watt, 16)
            sp.dma_start(cwv[:, :, :], t_in["L0_attn_cwv"].rearrange("(c p) d -> p c d", p=P)
                         ).then_inc(s_watt, 16)

            def load_block(n, i):
                sp.dma_start(xb[n % NXB][:, :], slots_dram[bass.ts(i, P), :]).then_inc(s_xb[n % NXB], 16)

            def run_blocks(v):
                sp.wait_ge(s_scat, 16 * NT * (v + 1))
                o = v * NBLK
                for i in range(NXB):
                    if v:
                        sp.wait_ge(s_xbTp, o + i - NXB + 1)
                    load_block(o + i, i)
                loops = (NBLK - NXB) // NXB
                with sp.Fori(0, loops) as r:
                    for k in range(NXB):
                        sp.wait_ge(s_xbTp, r * NXB + (o + k + 1))
                        load_block(o + k, r * NXB + (NXB + k))
                for i in range(NXB * (loops + 1), NBLK):
                    sp.wait_ge(s_xbTp, o + i - NXB + 1)
                    load_block(o + i, i)

            run_blocks(0)
            run_blocks(1)
            for b in range(NB):
                sp.wait_ge(s_x1, NB + b + 1)
                sp.dma_start(out_dram[b], tiles(X, b)).then_inc(s_out, 16)
            sp.wait_ge(s_out, 16 * NB)

        @block.gpsimd
        def _(g):
            g.memset(zero_rows[:, :], 0.0).then_inc(s_zero_set, 1)
            g.memset(ident[:, :], 0.0).then_inc(s_cmem, 1)
            g.memset(before[:, :], 1.0).then_inc(s_cmem, 1)
            g.memset(carry[:, :, :], 1.0).then_inc(s_cmem, 1)
            g.memset(ones[:, :], 1.0).then_inc(s_const, 1)
            g.memset(half_neg[:, :], -0.5).then_inc(s_const, 1)
            g.memset(ones_row[:, :], 1.0).then_inc(s_const, 1)
            g.memset(block_end[:, :], 0.0).then_inc(s_const, 1)
            g.iota(rank[:, :], pattern=[[-1, E]], base=E, channel_multiplier=0,
                   allow_small_or_imprecise_dtypes=True).then_inc(s_const, 1)
            g.iota(block_no[:, :], pattern=[[1, NBLK]], base=0, channel_multiplier=0,
                   allow_small_or_imprecise_dtypes=True).then_inc(s_const, 1)
            g.wait_ge(s_cmem, 3)
            g.affine_select(out=ident[:, :], in_=ident[:, :], compare_op=ALU.not_equal, fill=1.0,
                            base=0, pattern=[[-1, P]], channel_multiplier=1).then_inc(s_const, 1)
            g.affine_select(out=before[:, :], in_=before[:, :], compare_op=ALU.is_gt, fill=0.0,
                            base=0, pattern=[[1, P]], channel_multiplier=-1).then_inc(s_const, 1)
            g.affine_select(out=carry[:, :, :], in_=carry[:, :, :], compare_op=ALU.is_gt, fill=0.0,
                            base=0, pattern=[[0, E], [1, NT]], channel_multiplier=0
                            ).then_inc(s_const, 1)

            def rsqrt_ffn(v):
                for b in range(NB):
                    n = v * NB + b + 1
                    g.wait_ge(s_mv, n)
                    g.tensor_scalar(veps[:, J * b:J * b + J], mv[:, J * b:J * b + J, 1], EPS, None,
                                    ALU.add).then_inc(s_veps, 1)
                    g.wait_ge(s_veps, n)
                    g.tensor_tensor(rstd[:, J * b:J * b + J], veps[:, J * b:J * b + J],
                                    half_neg[:, 0:J], ALU.pow).then_inc(s_rstd, 1)

            def scatter(v):
                if v == 0:
                    g.wait_ge(s_zeroed, 16 * ((NBLK + 7) // 8))
                g.wait_ge(s_slot, v + 1)
                for b in range(NB):
                    g.wait_ge(s_xs, v * NB + b + 1)
                    for t in range(J * b, J * b + J):
                        g.indirect_dma_start(
                            out=slots_dram, out_offset=bass.IndirectOffsetOnAxis(ap=slot[:, t:t + 1], axis=0),
                            in_=xs[:, t, :], in_offset=None).then_inc(s_scat, 16)

            def gather(v):
                for k in range(NXB):
                    g.wait_ge(s_yst[k], 16 * len([i for i in range((v + 1) * NBLK) if i % NXB == k]))
                for t in range(NT):
                    g.indirect_dma_start(
                        out=yg[:, t, :], out_offset=None, in_=moe_dram,
                        in_offset=bass.IndirectOffsetOnAxis(ap=slot[:, t:t + 1], axis=0)
                    ).then_inc(s_yg[t // J], 16)

            def rwkv():
                def rstd_in(b):
                    i, n = b % 2, b + 1
                    g.wait_ge(sa["a_mv"], n)
                    g.tensor_scalar(a_veps[i][:, 0:J], a_mv[i][:, :, 1], EPS, None, ALU.add)
                    g.tensor_scalar(a_veps[i][:, J:2 * J], a_mv[i][:, :, 1], 1.0 + EPS, EPS * EPS,
                                    ALU.mult, ALU.add).then_inc(sa["a_veps"], 1)
                    g.wait_ge(sa["a_veps"], n)
                    if b >= 2:
                        g.wait_ge(sa["a_norm"], b - 1)
                    g.tensor_tensor(a_rstd[i][:, :], a_veps[i][:, :], half_neg[:, 0:2 * J], ALU.pow
                                    ).then_inc(sa["a_rstd"], 1)

                def rstd_mid(b):
                    i, n = b % 2, b + 1
                    g.wait_ge(sa["c_mv"], n)
                    g.tensor_scalar(c_veps[i][:, :], c_mv[i][:, :, 1], EPS, None, ALU.add
                                    ).then_inc(sa["c_veps"], 1)
                    g.wait_ge(sa["c_veps"], n)
                    if b >= 2:
                        g.wait_ge(sa["h2"], b - 1)
                    g.tensor_tensor(c_rstd[i][:, :], c_veps[i][:, :], half_neg[:, 0:J], ALU.pow
                                    ).then_inc(sa["c_rstd"], 1)

                def fall(b):
                    i, n = b % 2, b + 1
                    g.wait_ge(sa["peak"], n)
                    if b >= 2:
                        g.wait_ge(sa["aa"], b - 1)
                    g.tensor_tensor(d_old[i][:, :], peak[i][:, 0:T], peak[i][:, 1:T + 1], ALU.subtract
                                    ).then_inc(sa["d_old"], 1)

                def block_input(b):
                    i, n = b % 2, b + 1
                    g.wait_ge(sa["a_rstd"], n)
                    if b >= 2:
                        g.wait_ge(sa["x2"], b - 1)
                    for j in range(J):
                        m = g.tensor_scalar(a_in[i][:, j, :], X[:, J * b + j, :], a_mv[i][:, j, 0:1],
                                            a_rstd[i][:, j:j + 1], ALU.subtract, ALU.mult)
                    m.then_inc(sa["a_in"], 1)

                def change(b):
                    i, n = b % 2, b + 1
                    g.wait_ge(sa["h2T"], n)
                    if b >= 2:
                        g.wait_ge(sa["mix_r"], b - 1)
                    g.tensor_tensor(dh[i][:, :], h2T[i][:, 1:T + 1], h2T[i][:, 0:T], ALU.subtract
                                    ).then_inc(sa["dh"], 1)

                def old_parts(b):
                    i, n = b % 2, b + 1
                    g.wait_ge(sa["e1"], n)
                    g.wait_ge(sa["aa"], n)
                    if b >= 2:
                        g.wait_ge(sa["num"], b - 1)
                    g.tensor_tensor(num_old[i][:, :], e1[i][:, :], aa[i][:, 0:T], ALU.mult
                                    ).then_inc(sa["num_old"], 1)
                    g.wait_ge(sa["bb"], n)
                    if b >= 2:
                        g.wait_ge(sa["wkv"], b - 1)
                    g.tensor_tensor(den_old[i][:, :], e1[i][:, :], bb[i][:, 0:T], ALU.mult
                                    ).then_inc(sa["den_old"], 1)
                    g.wait_ge(sa["den_old"], n)
                    g.wait_ge(sa["e2"], n)
                    g.tensor_tensor(den_old[i][:, :], den_old[i][:, :], e2[i][:, :], ALU.add
                                    ).then_inc(sa["den"], 1)

                def two_inputs(b):
                    i, n = b % 2, b + 1
                    g.wait_ge(sa["x2"], n)
                    g.wait_ge(sa["a_in"], n)
                    g.tensor_tensor(flat(X, b), flat(X, b), x2[i][:, :, :].rearrange("p t d -> p (t d)"),
                                    ALU.add).then_inc(sa["x12"], 1)

                pipelined([(fall, 1), (rstd_mid, 2), (rstd_in, 0), (old_parts, 1), (two_inputs, 2),
                           (change, 2), (block_input, 0)])

            for i in range(2):
                g.memset(h1T[i][:, 0:1], 0.0)
                g.memset(h2T[i][:, 0:1], 0.0)
                g.memset(aa[i][:, 0:1], 0.0)
                g.memset(bb[i][:, 0:1], 0.0)
                last = g.memset(peak[i][:, 0:1], LOWEST)
            last.then_inc(s_edge, 1)
            rsqrt_ffn(0)
            scatter(0)
            gather(0)
            rwkv()
            rsqrt_ffn(1)
            scatter(1)
            gather(1)

        @block.scalar
        def _(a):
            a.wait_ge(s_wtp, 1)
            a.copy(w_gateT[:, :, :].rearrange("p c f -> p (c f)"), bank[2][:, 0:FS])
            a.copy(w_upT[:, :, :].rearrange("p c f -> p (c f)"), bank[3][:, 0:FS])
            a.copy(w_downT[:, :, :].rearrange("p c d -> p (c d)"), bank[4][:, 0:SC * D])
            a.copy(w_routerT[:, :], bank[5][:, 0:E]).then_inc(s_wt, 1)

            def ffn_front(v):
                for b in range(NB):
                    a.wait_ge(s_xnTp, v * NB + b + 1)
                    a.copy(xnT[:, b, :], bank[b % 2][:, :]).then_inc(s_xnT, 1)
                a.wait_ge(s_best, v + 1)
                a.activation(th_score[:, :], best[:, :], ACT.Tanh, scale=0.5).then_inc(s_thsc, 1)
                for b in range(NB):
                    if b == 0:
                        a.wait_ge(s_score, v + 1)
                    if v:
                        a.wait_ge(s_x1, NB * v)
                    for t in range(J * b, J * b + J):
                        i = a.activation(xs[:, t, :], xn[:, t, :], ACT.Copy, scale=score[:, t:t + 1])
                    i.then_inc(s_xs, 1)
                for b in range(NB):
                    for c in range(SC):
                        n = (v * NB + b) * SC + c
                        a.wait_ge(s_sgu, n + 1)
                        if n >= SC:
                            a.wait_ge(s_sact, n + 1 - SC)
                        a.activation(sg[c][:, :], bank[2 + 2 * c][:, :], ACT.Silu).then_inc(s_ssilu, 1)

            def moe(v):
                def silu(i, k):
                    n = v * NBLK + i
                    a.wait_ge(s_mgu, n + 1)
                    a.activation(mg[k % 2][:, :], bank[2 + k % 2][:, 0:FM], ACT.Silu).then_inc(s_mg, 1)

                def turn(i, k):
                    n = v * NBLK + i
                    a.wait_ge(s_maTp, n + 1)
                    a.copy(maT[k % 2][:, :, :].rearrange("p c f -> p (c f)"),
                           bank[4 + k % 2][:, 0:FM]).then_inc(s_maT, 1)

                def store(i, k):
                    a.wait_ge(s_yb, v * NBLK + i + 1)
                    a.dma_start(moe_dram[bass.ts(i, P), :], yb[k % NXB][:, :]
                                ).then_inc(s_yst[k % NXB], 16)

                o = v * NBLK
                LAG = 3
                for i in range(LAG + 1):
                    silu(i, o + i)
                    if i:
                        turn(i - 1, o + i - 1)
                store(0, o)
                first = LAG + 1
                loops = (NBLK - first) // NXB
                with a.Fori(0, loops) as r:
                    for k in range(NXB):
                        i = r * NXB + (first + k)
                        silu(i, o + first + k)
                        turn(i - 1, o + first + k - 1)
                        store(i - LAG, o + first + k - LAG)
                for i in range(first + loops * NXB, NBLK + LAG):
                    if i < NBLK:
                        silu(i, o + i)
                    if i <= NBLK:
                        turn(i - 1, o + i - 1)
                    store(i - LAG, o + i - LAG)

            def rwkv():
                def exp_row(b, name, out_, in_, scale=1.0, bias=0.0):
                    a.activation(out_[b % 2][:, :], in_[b % 2][:, :], ACT.Exp, scale=scale, bias=bias
                                 ).then_inc(sa[name], 1)

                def turned_in(b):
                    i, n = b % 2, b + 1
                    a.wait_ge(sa["h1Tp"], n)
                    if b == 0:
                        a.wait_ge(s_watt, 16 * (len(VEC) + 7))
                        a.wait_ge(s_edge, 1)
                    if b >= 2:
                        a.wait_ge(sa["r"], b - 1)
                    a.activation(h1T[i][:, 1:T + 1], bank[0][:, :], ACT.Identity,
                                 scale=vec["ln1_g"][:, 0:1], bias=vec["ln1_b"][:, 0:1]
                                 ).then_inc(sa["h1T"], 1)

                def turned_mid(b):
                    i, n = b % 2, b + 1
                    a.wait_ge(sa["h2Tp"], n)
                    if b >= 2:
                        a.wait_ge(sa["mix_r"], b - 1)
                    a.activation(h2T[i][:, 1:T + 1], bank[0][:, :], ACT.Identity,
                                 scale=vec["ln2_g"][:, 0:1], bias=vec["ln2_b"][:, 0:1]
                                 ).then_inc(sa["h2T"], 1)

                def state_exps(b):
                    n = b + 1
                    a.wait_ge(sa["d_now"], n)
                    if b >= 2:
                        a.wait_ge(sa["bb"], b - 1)
                    exp_row(b, "e2b", e2b, d_now)
                    a.wait_ge(sa["d_old"], n)
                    if b == 0:
                        a.wait_ge(s_prep, 1)
                    exp_row(b, "e1b", e1b, d_old, bias=decay[:, 0:1])

                def out_exps(b):
                    i, n = b % 2, b + 1
                    a.wait_ge(sa["d_out"], n)
                    if b >= 2:
                        a.wait_ge(sa["den"], b - 1)
                        a.wait_ge(sa["num_new"], b - 1)
                    a.activation(d_neg[i][:, :], d_out[i][:, :], ACT.Relu, scale=-1.0).then_inc(sa["d_neg"], 1)
                    a.wait_ge(sa["d_neg"], n)
                    a.activation(d_pos[i][:, :], d_out[i][:, :], ACT.Relu).then_inc(sa["d_pos"], 1)
                    exp_row(b, "e2", e2, d_neg, scale=-1.0)
                    a.wait_ge(sa["d_pos"], n)
                    exp_row(b, "e1", e1, d_pos, scale=-1.0)

                def receptance(b):
                    a.wait_ge(sa["r"], b + 1)
                    if b >= 2:
                        a.wait_ge(sa["rw"], b - 1)
                    a.activation(th_r[b % 2][:, :], bank[3][:, :], ACT.Tanh, scale=0.5
                                 ).then_inc(sa["th_r"], 1)

                def squared_relus(b):
                    def square(c):
                        a.wait_ge(sa["pos_kk"], CC * b + c + 1)
                        a.activation(kk[c][:, :], kk[c][:, :], ACT.Square).then_inc(sa["kk"], 1)
                    for c in range(CC):
                        a.wait_ge(sa["cwk"], CC * b + c + 1)
                        if b >= 1:
                            a.wait_ge(sa["cwv"], b)
                        a.activation(kk[c][:, :], bank[6 + c % 2][:, :], ACT.Relu
                                     ).then_inc(sa["pos_kk"], 1)
                        if c:
                            square(c - 1)
                    square(CC - 1)

                def gate(b):
                    a.wait_ge(sa["rr"], b + 1)
                    if b >= 2:
                        a.wait_ge(sa["rcv"], b - 1)
                    a.activation(th_rr[b % 2][:, :], bank[4][:, :], ACT.Tanh, scale=0.5
                                 ).then_inc(sa["th_rr"], 1)

                pipelined([(state_exps, 1), (out_exps, 1), (receptance, 1), (turned_mid, 2),
                           (turned_in, 0), (squared_relus, 2), (gate, 2)])

            ffn_front(0)
            moe(0)
            a.wait_ge(s_watt, 16 * (len(VEC) + 7))
            a.activation(decay_exp[:, :], vec["time_decay"][:, :], ACT.Exp).then_inc(s_dexp, 1)
            rwkv()
            ffn_front(1)
            moe(1)

        @block.vector
        def _(d):
            def norm_ffn(v, b):
                n = v * NB + b + 1
                if v == 0:
                    d.wait_ge(s_x[b], 16)
                else:
                    d.wait_ge(sa["x_att"], b + 1)
                for t in range(J * b, J * b + J):
                    i = d.bn_stats(stats[:, t, :], X[:, t, :])
                i.then_inc(s_stats, 1)
                d.wait_ge(s_stats, n)
                for t in range(J * b, J * b + J):
                    i = d.bn_aggr(mv[:, t, :], stats[:, t, :])
                i.then_inc(s_mv, 1)

            def scale_ffn(v, b):
                d.wait_ge(s_rstd, v * NB + b + 1)
                for t in range(J * b, J * b + J):
                    i = d.tensor_scalar(xn[:, t, :], X[:, t, :], mv[:, t, 0:1], rstd[:, t:t + 1],
                                        ALU.subtract, ALU.mult)
                i.then_inc(s_xn, 1)

            def route(v):
                c = [v * 12]

                def done(ins):
                    c[0] += 1
                    ins.then_inc(s_rt, 1)
                    d.wait_ge(s_rt, c[0])

                logit = bank[7][:, 0:NT * E].rearrange("p (t e) -> p t e", e=E)
                d.wait_ge(s_logit, v * NB + NB)
                d.tensor_reduce(best[:, :], logit, AX.X, ALU.max).then_inc(s_best, 1)
                d.wait_ge(s_best, v + 1)
                done(d.tensor_tensor(is_best[:, :, :], logit,
                                     best[:, :].unsqueeze(2).to_broadcast([P, NT, E]), ALU.is_ge))
                done(d.tensor_tensor(ranked[:, :, :], is_best[:, :, :],
                                     rank[:, :].unsqueeze(1).to_broadcast([P, NT, E]), ALU.mult))
                done(d.tensor_reduce(top_rank[:, :], ranked[:, :, :], AX.X, ALU.max))
                d.tensor_tensor(onehot[:, :, :], rank[:, :].unsqueeze(1).to_broadcast([P, NT, E]),
                                top_rank[:, :].unsqueeze(2).to_broadcast([P, NT, E]),
                                ALU.is_equal).then_inc(s_onehot, 1)
                d.wait_ge(s_thsc, v + 1)
                d.tensor_scalar(score[:, :], th_score[:, :], 1.0, 0.5, ALU.add, ALU.mult
                                ).then_inc(s_score, 1)
                total = bank[6][:, 0:NT * E].rearrange("p (t e) -> p e t", e=E)
                d.wait_ge(s_count, v + 1)
                done(d.tensor_reduce(count[:, :], total, AX.X, ALU.add))
                done(d.tensor_scalar(blocks_f[:, :], count[:, :], (P - 1) / 2.0, 1.0 / P, ALU.add,
                                     ALU.mult))
                done(d.tensor_scalar(blocks[:, :], blocks_f[:, :], ROUND, -ROUND, ALU.add, ALU.add))
                done(d.tensor_tensor_scan(block_end[:, 1:E + 1], ones_row[:, :], blocks[:, :], 0.0,
                                          ALU.mult, ALU.add))
                d.tensor_copy(steps[:, :, 1:NT], total[:, :, 0:NT - 1])
                done(d.tensor_scalar(steps[:, :, 0], block_end[:, 0:E], float(P), None, ALU.mult))
                done(d.tensor_tensor_scan(tile_start[:, :, :].rearrange("p e t -> p (e t)"),
                                          carry[:, :, :].rearrange("p e t -> p (e t)"),
                                          steps[:, :, :].rearrange("p e t -> p (e t)"), 0.0,
                                          ALU.mult, ALU.add))
                done(d.tensor_tensor(slot_all[:, :, :],
                                     tile_start[:, :, :].rearrange("p e t -> p t e"),
                                     bank[5][:, 0:NT * E].rearrange("p (t e) -> p t e", e=E), ALU.add))
                done(d.tensor_tensor(slot_sel[:, :, :], slot_all[:, :, :], onehot[:, :, :], ALU.mult))
                done(d.tensor_reduce(slot_f[:, :], slot_sel[:, :, :], AX.X, ALU.add))
                d.tensor_copy(slot[:, :], slot_f[:, :]).then_inc(s_slot, 1)
                assert c[0] == 12 * (v + 1), c
                d.tensor_tensor(past[:, :, :],
                                block_no[:, :].unsqueeze(2).to_broadcast([1, NBLK, E - 1]),
                                block_end[0:1, 1:E].unsqueeze(1).to_broadcast([1, NBLK, E - 1]),
                                ALU.is_ge).then_inc(s_bexp, 1)
                d.wait_ge(s_bexp, 3 * v + 1)
                d.tensor_reduce(block_expert_f[:, :], past[:, :, :], AX.X, ALU.add).then_inc(s_bexp, 1)
                d.wait_ge(s_bexp, 3 * v + 2)
                d.tensor_scalar(block_row[:, :], block_expert_f[:, :], float(ROW), None, ALU.mult
                                ).then_inc(s_bexp, 1)

            def shared(v):
                def act_chunk(b, c):
                    n = (v * NB + b) * SC + c
                    d.wait_ge(s_ssilu, n + 1)
                    if n >= SC:
                        d.wait_ge(s_sdn, v * NB + b)
                    d.tensor_tensor(act[c][:, :], sg[c][:, :], bank[3 + 2 * c][:, :], ALU.mult
                                    ).then_inc(s_sact, 1)

                def residual(b):
                    d.wait_ge(s_sdn, v * NB + b + 1)
                    d.scalar_tensor_tensor(out=flat(X, b), in0=bank[6][:, :], scalar=0.5,
                                           in1=flat(X, b), op0=ALU.mult, op1=ALU.add
                                           ).then_inc(s_sres, 1)
                for b in range(NB):
                    act_chunk(b, 0)
                    if b:
                        residual(b - 1)
                    act_chunk(b, 1)
                residual(NB - 1)

            def moe(v):
                def xT(i, k):
                    n = v * NBLK + i
                    d.wait_ge(s_xbTp, n + 1)
                    d.tensor_copy(xbT[k % 2][:, :], bank[k % 2][:, 0:P]
                                  ).then_inc(s_xbT, 1)

                def gate(i, k):
                    n = v * NBLK + i
                    d.wait_ge(s_mg, n + 1)
                    d.tensor_tensor(ma[k % 2][:, :], mg[k % 2][:, :], bank[2 + k % 2][:, FM:2 * FM],
                                    ALU.mult).then_inc(s_ma, 1)

                def y(i, k):
                    n = v * NBLK + i
                    d.wait_ge(s_my, n + 1)
                    if n >= NXB:
                        d.wait_ge(s_yst[k % NXB], 16 * (n // NXB))
                    d.tensor_scalar(yb[k % NXB][:, :], bank[6 + k % 2][:, 0:P], 0.5,
                                    None, ALU.mult).then_inc(s_yb, 1)

                o = v * NBLK
                def slot(i):
                    if i + 2 < NBLK:
                        xT(i + 2, o + i + 2)
                    if 0 <= i < NBLK:
                        gate(i, o + i)
                    if i >= 2:
                        y(i - 2, o + i - 2)

                first = NXB + 2
                loops = (NBLK - 2 - first) // NXB
                for i in range(-2, first):
                    slot(i)
                with d.Fori(0, loops) as r:
                    for k in range(NXB):
                        i = r * NXB + (first + k)
                        n = o + first + k
                        xT(i + 2, n + 2)
                        gate(i, n)
                        d.wait_ge(s_my, i + (o - 1))
                        d.wait_ge(s_yst[(n - 2) % NXB], r * 16 + 16 * ((n - 2) // NXB))
                        d.tensor_scalar(yb[(n - 2) % NXB][:, :], bank[6 + n % 2][:, 0:P], 0.5,
                                        None, ALU.mult).then_inc(s_yb, 1)
                for i in range(first + loops * NXB, NBLK + 2):
                    slot(i)

            def ffn(v):
                for b in range(NB):
                    norm_ffn(v, b)
                    if b:
                        scale_ffn(v, b - 1)
                scale_ffn(v, NB - 1)
                route(v)
                shared(v)
                moe(v)

            def add_moe(v):
                for b in range(NB):
                    d.wait_ge(s_yg[b], 16 * J * (v + 1))
                    d.tensor_tensor(flat(X, b), flat(X, b), flat(yg, b), ALU.add).then_inc(s_x1, 1)

            def prepare():
                d.wait_ge(s_watt, 16 * (len(VEC) + 7))
                for j, m in enumerate(WMIX):
                    i = d.tensor_scalar(one_minus[:, j:j + 1], vec["tm_mix_" + m][:, :], -1.0, 1.0,
                                        ALU.mult, ALU.add)
                i.then_inc(s_omix, 1)
                d.wait_ge(s_omix, 1)
                for j, m in enumerate(WMIX):
                    d.tensor_scalar(w_now[m][:, :], w_tm[m][:, :], vec["tm_mix_" + m][:, 0:1], None, ALU.mult)
                    i = d.tensor_scalar(w_prev[m][:, :], w_tm[m][:, :], one_minus[:, j:j + 1], None, ALU.mult)
                i.then_inc(s_wmix, 1)

            def prepare_decay():
                d.wait_ge(s_dexp, 1)
                d.tensor_scalar(decay[:, :], decay_exp[:, :], -1.0, None, ALU.mult).then_inc(s_prep, 1)
                d.wait_ge(s_prep, 1)
                d.tensor_copy(decay_row[:, :], decay[:, 0:1].to_broadcast([P, T])).then_inc(s_prep, 1)
                d.wait_ge(s_prep, 2)

            def rwkv():
                def wait(name, n):
                    if n > 0:
                        d.wait_ge(sa[name], n)

                def inputs(b):
                    i, n = b % 2, b + 1
                    d.wait_ge(s_yg[b], 16 * J)
                    d.tensor_tensor(flat(X, b), flat(X, b), flat(yg, b), ALU.add).then_inc(s_x1, 1)
                    d.wait_ge(s_x1, n)
                    for j in range(J):
                        m = d.bn_stats(a_stats[i][:, j, :], X[:, J * b + j, :])
                    m.then_inc(sa["a_stats"], 1)
                    d.wait_ge(sa["a_stats"], n)
                    wait("a_in", b - 1)
                    for j in range(J):
                        m = d.bn_aggr(a_mv[i][:, j, :], a_stats[i][:, j, :])
                    m.then_inc(sa["a_mv"], 1)

                def mid(b):
                    i, n = b % 2, b + 1
                    d.wait_ge(sa["wo"], n)
                    d.wait_ge(sa["a_in"], n)
                    wait("x12", b - 1)
                    d.scalar_tensor_tensor(out=x2[i][:, :, :].rearrange("p t d -> p (t d)"),
                                           in0=bank[4][:, :], scalar=0.5,
                                           in1=a_in[i][:, :, :].rearrange("p t d -> p (t d)"),
                                           op0=ALU.mult, op1=ALU.add).then_inc(sa["x2"], 1)
                    d.wait_ge(sa["x2"], n)
                    for j in range(J):
                        m = d.bn_stats(c_stats[i][:, j, :], x2[i][:, j, :])
                    m.then_inc(sa["c_stats"], 1)
                    d.wait_ge(sa["c_stats"], n)
                    wait("c_veps", b - 1)
                    for j in range(J):
                        m = d.bn_aggr(c_mv[i][:, j, :], c_stats[i][:, j, :])
                    m.then_inc(sa["c_mv"], 1)

                def norm_in(b):
                    i, n = b % 2, b + 1
                    d.wait_ge(sa["a_rstd"], n)
                    wait("h1Tp", b - 1)
                    for j in range(J):
                        m = d.tensor_scalar(h1[i][:, j, :], X[:, J * b + j, :], a_mv[i][:, j, 0:1],
                                            a_rstd[i][:, J + j:J + j + 1], ALU.subtract, ALU.mult)
                    m.then_inc(sa["a_norm"], 1)

                def norm_mid(b):
                    i, n = b % 2, b + 1
                    d.wait_ge(sa["c_rstd"], n)
                    wait("h2Tp", b - 1)
                    for j in range(J):
                        m = d.tensor_scalar(h2[i][:, j, :], x2[i][:, j, :], c_mv[i][:, j, 0:1],
                                            c_rstd[i][:, j:j + 1], ALU.subtract, ALU.mult)
                    m.then_inc(sa["h2"], 1)

                def peaks(b):
                    i, n = b % 2, b + 1
                    d.wait_ge(sa["k"], n)
                    if b == 0:
                        prepare_decay()
                        d.wait_ge(s_edge, 1)
                    wait("d_old", b - 1)
                    d.tensor_tensor_scan(peak[i][:, 1:T + 1], decay_row[:, :], bank[1][:, :], LOWEST,
                                         ALU.add, ALU.max).then_inc(sa["peak"], 1)
                    d.wait_ge(sa["peak"], n)
                    d.tensor_tensor(d_now[i][:, :], bank[1][:, :], peak[i][:, 1:T + 1], ALU.subtract
                                    ).then_inc(sa["d_now"], 1)
                    wait("den_old", b - 1)
                    d.scalar_tensor_tensor(out=d_out[i][:, :], in0=bank[1][:, :],
                                           scalar=vec["time_first"][:, 0:1], in1=peak[i][:, 0:T],
                                           op0=ALU.add, op1=ALU.subtract).then_inc(sa["d_out"], 1)

                def mixes(b):
                    i, n = b % 2, b + 1
                    d.wait_ge(sa["dh"], n)
                    wait("cwk", CC * (b - 1))
                    d.scalar_tensor_tensor(out=mix_k[i][:, :], in0=dh[i][:, :],
                                           scalar=vec["cm_mix_k"][:, 0:1], in1=h2T[i][:, 0:T],
                                           op0=ALU.mult, op1=ALU.add).then_inc(sa["mix_k"], 1)
                    wait("rr", b - 1)
                    d.scalar_tensor_tensor(out=mix_r[i][:, :], in0=dh[i][:, :],
                                           scalar=vec["cm_mix_r"][:, 0:1], in1=h2T[i][:, 0:T],
                                           op0=ALU.mult, op1=ALU.add).then_inc(sa["mix_r"], 1)

                def states(b):
                    i, n = b % 2, b + 1
                    d.wait_ge(sa["e2b"], n)
                    d.wait_ge(sa["v"], n)
                    d.tensor_tensor(kv[i][:, :], e2b[i][:, :], bank[2][:, :], ALU.mult
                                    ).then_inc(sa["kv"], 1)
                    d.wait_ge(sa["e1b"], n)
                    wait("den", b - 1)
                    d.tensor_tensor_scan(bb[i][:, 1:T + 1], e1b[i][:, :], e2b[i][:, :], 0.0,
                                         ALU.mult, ALU.add).then_inc(sa["bb"], 1)
                    d.wait_ge(sa["kv"], n)
                    wait("num_old", b - 1)
                    d.tensor_tensor_scan(aa[i][:, 1:T + 1], e1b[i][:, :], kv[i][:, :], 0.0,
                                         ALU.mult, ALU.add).then_inc(sa["aa"], 1)
                    d.wait_ge(sa["e2"], n)
                    wait("wo", b - 1)
                    d.tensor_tensor(num_new[i][:, :], e2[i][:, :], bank[2][:, :], ALU.mult
                                    ).then_inc(sa["num_new"], 1)

                def divide(b):
                    i, n = b % 2, b + 1
                    d.wait_ge(sa["num_old"], n)
                    d.wait_ge(sa["num_new"], n)
                    d.tensor_tensor(num_new[i][:, :], num_new[i][:, :], num_old[i][:, :], ALU.add
                                    ).then_inc(sa["num"], 1)
                    d.wait_ge(sa["den"], n)
                    d.reciprocal(den_old[i][:, :], den_old[i][:, :]).then_inc(sa["rden"], 1)
                    d.wait_ge(sa["rden"], n)
                    d.tensor_tensor(num_new[i][:, :], num_new[i][:, :], den_old[i][:, :], ALU.mult
                                    ).then_inc(sa["wkv"], 1)
                    d.wait_ge(sa["wkv"], n)
                    d.wait_ge(sa["th_r"], n)
                    d.scalar_tensor_tensor(out=rw[i][:, :], in0=th_r[i][:, :], scalar=1.0,
                                           in1=num_new[i][:, :], op0=ALU.add, op1=ALU.mult
                                           ).then_inc(sa["rw"], 1)

                def outputs(b):
                    i, n = b % 2, b + 1
                    d.wait_ge(sa["th_rr"], n)
                    d.wait_ge(sa["cwv"], n)
                    d.scalar_tensor_tensor(out=th_rr[i][:, :], in0=th_rr[i][:, :], scalar=1.0,
                                           in1=bank[5][:, :], op0=ALU.add, op1=ALU.mult
                                           ).then_inc(sa["rcv"], 1)
                    d.wait_ge(sa["rcv"], n)
                    d.wait_ge(sa["x12"], n)
                    d.scalar_tensor_tensor(out=flat(X, b), in0=th_rr[i][:, :], scalar=0.5,
                                           in1=flat(X, b), op0=ALU.mult, op1=ALU.add
                                           ).then_inc(sa["x_att"], 1)

                pipelined([(peaks, 1), (mid, 2), (inputs, 0), (states, 1), (norm_mid, 2), (outputs, 3),
                           (norm_in, 0), (mixes, 2), (divide, 1)])

            ffn(0)
            prepare()
            rwkv()
            ffn(1)
            add_moe(1)

        @block.tensor
        def _(t):
            t.wait_ge(s_const, 9)
            t.wait_ge(s_wsh, 64)
            for c in range(SC):
                t.transpose(bank[2][:, c * P:c * P + P], w_gate_raw[:, c, :], ident[:, :])
                t.transpose(bank[3][:, c * P:c * P + P], w_up_raw[:, c, :], ident[:, :])
                t.transpose(bank[4][:, c * P:c * P + P], w_down_raw[:, c * P:c * P + P], ident[:, :])
            t.transpose(bank[5][:, 0:E], w_router_raw[:, :], ident[0:E, 0:E]).then_inc(s_wtp, 1)

            def front(v):
                def turn(b):
                    t.wait_ge(s_xn, v * NB + b + 1)
                    if v * NB + b >= 2:
                        t.wait_ge(s_xnT, v * NB + b - 1)
                    for j in range(J):
                        m = t.transpose(bank[b % 2][:, j * P:j * P + P], xn[:, J * b + j, :], ident[:, :])
                    m.then_inc(s_xnTp, 1)

                def router(b):
                    t.wait_ge(s_xnT, v * NB + b + 1)
                    if v == 0 and b == 0:
                        t.wait_ge(s_wt, 1)
                    for j in range(J):
                        k = J * b + j
                        m = t.matmul(bank[7][:, k * E:k * E + E], xnT[:, b, j * P:j * P + P],
                                     w_routerT[:, :], start=True, stop=True)
                    m.then_inc(s_logit, 1)

                if v:
                    t.wait_ge(s_xbT, v * NBLK)
                for b in range(NB):
                    turn(b)
                    if b:
                        router(b - 1)
                router(NB - 1)

            def count_tokens(v):
                t.wait_ge(s_onehot, v + 1)
                oh = onehot[:, :, :].rearrange("p t e -> p (t e)")
                t.matmul(bank[6][:, 0:NT * E], ones[:, :], oh, start=True, stop=True)
                t.matmul(bank[5][:, 0:NT * E], before[:, :], oh, start=True, stop=True
                         ).then_inc(s_count, 1)

            def shared(v):
                def gate_up_chunk(b, c):
                    n = (v * NB + b) * SC + c
                    if n >= SC:
                        t.wait_ge(s_sact, n + 1 - SC)
                    t.matmul(bank[2 + 2 * c][:, :], w_gateT[:, c, :], xnT[:, b, :], start=True, stop=True)
                    t.matmul(bank[3 + 2 * c][:, :], w_upT[:, c, :], xnT[:, b, :], start=True, stop=True
                             ).then_inc(s_sgu, 1)

                def down_tiles(b):
                    t.wait_ge(s_sact, (v * NB + b + 1) * SC)
                    if v * NB + b:
                        t.wait_ge(s_sres, v * NB + b)
                    for j in range(J):
                        for c in range(SC):
                            m = t.matmul(bank[6][:, j * P:j * P + P], act[c][:, j * P:j * P + P],
                                         w_downT[:, c, :], start=(c == 0), stop=(c == SC - 1))
                    m.then_inc(s_sdn, 1)

                for b in range(NB):
                    gate_up_chunk(b, 0)
                    if b == 0:
                        count_tokens(v)
                        t.wait_ge(s_slot, v + 1)
                    gate_up_chunk(b, 1)
                    if b:
                        down_tiles(b - 1)
                down_tiles(NB - 1)

            def moe(v):
                o = v * NBLK

                def turn_x(n, landed):
                    t.wait_ge(s_xb[n % NXB], landed)
                    t.transpose(bank[n % 2][:, 0:P], xb[n % NXB][:, :], ident[:, :]).then_inc(s_xbTp, 1)

                def gate_up_block(n, i, row):
                    t.wait_ge(s_xbT, i + (o + 1))
                    t.matmul(bank[2 + n % 2][:, :], xbT[n % 2][:, :], experts[:, bass.ds(row, F2)],
                             start=True, stop=True).then_inc(s_mgu, 1)

                def turn_a(n, i):
                    t.wait_ge(s_ma, i + (o + 1))
                    for c in range(FC):
                        m = t.transpose(bank[4 + n % 2][:, c * P:c * P + P], ma[n % 2][:, c * P:c * P + P],
                                        ident[:, :])
                    m.then_inc(s_maTp, 1)

                def down_block(n, i, row):
                    t.wait_ge(s_maT, i + (o + 1))
                    for c in range(FC):
                        m = t.matmul(bank[6 + n % 2][:, 0:P], maT[n % 2][:, c, :],
                                     experts[:, bass.ds(row + (F2 + c * D), D)],
                                     start=(c == 0), stop=(c == FC - 1))
                    m.then_inc(s_my, 1)

                def rows(i, n):
                    _, values = nc.values_load_multi_w_load_instructions(
                        block_row[0:1, bass.ds(i, n)], engines=[mybir.EngineType.PE],
                        min_val=0, max_val=(E - 1) * ROW, 
                        skip_runtime_bounds_check_because="VectorE counted at most E - 1 experts")
                    return values

                def slot(i):
                    if i + 2 < NBLK:
                        turn_x(o + i + 2, 16 * ((o + i + 2) // NXB + 1))
                    if 0 <= i + 1 < NBLK:
                        gate_up_block(o + i + 1, i + 1, rows(i + 1, 1)[0])
                    if 0 <= i < NBLK:
                        turn_a(o + i, i)
                    if i == NBLK:
                        t.wait_ge(s_yb, o + i - 2)
                    if 0 <= i - 1:
                        down_block(o + i - 1, i - 1, rows(i - 1, 1)[0])

                t.wait_ge(s_bexp, 3 * v + 3)
                t.wait_ge(s_sres, (v + 1) * NB)
                if v == 0:
                    t.wait_ge(s_wmoe, 16 * (E // 4 + E))
                first = 1
                loops = (NBLK - 2 - first) // NXB
                for i in range(-2, first):
                    slot(i)
                with t.Fori(0, loops) as r:
                    row = rows(r * NXB + (first - 1), NXB + 2)
                    for k in range(NXB):
                        i = r * NXB + (first + k)
                        n = o + first + k
                        turn_x(n + 2, r * 16 + 16 * ((n + 2) // NXB + 1))
                        gate_up_block(n + 1, i + 1, row[k + 2])
                        turn_a(n, i)
                        down_block(n - 1, i - 1, row[k])
                for i in range(first + loops * NXB, NBLK + 1):
                    slot(i)

            def ffn(v):
                front(v)
                shared(v)
                moe(v)

            def rwkv():
                def wait(name, n):
                    if n > 0:
                        t.wait_ge(sa[name], n)

                def turn(b, bank_, src, name):
                    for j in range(J):
                        m = t.transpose(bank_[:, j * P:j * P + P], src[b % 2][:, j, :], ident[:, :])
                    m.then_inc(sa[name], 1)

                def turn_in(b):
                    t.wait_ge(sa["a_norm"], b + 1)
                    if b == 0:
                        t.wait_ge(s_yb, NBLK)
                    wait("h2T", b - 1)
                    turn(b, bank[0], h1, "h1Tp")

                def turn_mid(b):
                    t.wait_ge(sa["h2"], b + 1)
                    wait("h1T", min(b + 2, NB))
                    turn(b, bank[0], h2, "h2Tp")

                def kvr(b):
                    i = b % 2
                    t.wait_ge(sa["h1T"], b + 1)
                    if b == 0:
                        t.wait_ge(s_wmix, 1)
                    for m, bk, free in (("k", 1, "d_out"), ("v", 2, "num_new"), ("r", 3, "th_r")):
                        wait(free, b)
                        t.matmul(bank[bk][:, :], w_now[m][:, :], h1T[i][:, 1:T + 1], start=True, stop=False)
                        t.matmul(bank[bk][:, :], w_prev[m][:, :], h1T[i][:, 0:T], start=False, stop=True
                                 ).then_inc(sa[m], 1)

                def channel(b):
                    i = b % 2
                    t.wait_ge(sa["mix_k"], b + 1)
                    for c in range(CC):
                        wait("pos_kk", CC * b + c - 1)
                        t.matmul(bank[6 + c % 2][:, :], cwk[:, c * P:c * P + P], mix_k[i][:, :],
                                 start=True, stop=True).then_inc(sa["cwk"], 1)
                    t.wait_ge(sa["mix_r"], b + 1)
                    t.wait_ge(sa["x2"], b + 1)
                    for j in range(J):
                        m = t.matmul(bank[4][:, j * P:j * P + P], mix_r[i][:, j * P:j * P + P], cwr[:, :],
                                     start=True, stop=True)
                    m.then_inc(sa["rr"], 1)

                def channel_out(b):
                    t.wait_ge(sa["kk"], CC * (b + 1))
                    wait("rcv", b)
                    for j in range(J):
                        for c in range(CC):
                            m = t.matmul(bank[5][:, j * P:j * P + P], kk[c][:, j * P:j * P + P],
                                         cwv[:, c, :], start=(c == 0), stop=(c == CC - 1))
                    m.then_inc(sa["cwv"], 1)

                def project(b):
                    t.wait_ge(sa["rw"], b + 1)
                    wait("th_rr", b)
                    for j in range(J):
                        m = t.matmul(bank[4][:, j * P:j * P + P], rw[b % 2][:, j * P:j * P + P], wo[:, :],
                                     start=True, stop=True)
                    m.then_inc(sa["wo"], 1)

                pipelined([(project, 2), (channel_out, 3), (turn_mid, 2), (turn_in, 0), (kvr, 0),
                           (channel, 2)])

            ffn(0)
            rwkv()
            ffn(1)


_INS = ["L0_attn_x", "L0_attn_ln1_g", "L0_attn_ln1_b", "L0_attn_ln2_g", "L0_attn_ln2_b",
        "L0_attn_tm_mix_k", "L0_attn_tm_mix_v", "L0_attn_tm_mix_r", "L0_attn_time_decay",
        "L0_attn_time_first", "L0_attn_wk", "L0_attn_wv", "L0_attn_wr", "L0_attn_wo",
        "L0_attn_cm_mix_k", "L0_attn_cm_mix_r", "L0_attn_cwk", "L0_attn_cwv", "L0_attn_cwr",
        "L0_ffn_w_router", "L0_ffn_gate_up_proj", "L0_ffn_down_proj", "L0_ffn_w_gate",
        "L0_ffn_w_up", "L0_ffn_w_down"]


def kernel(**inputs):
    import numpy as _np
    import concourse.bacc as _bacc
    from concourse import mybir as _mybir
    from concourse.bass_utils import run_bass_kernel_spmd as _run

    nc = _bacc.Bacc("TRN2", target_bir_lowering=False, num_devices=1)
    arrays, args = {}, {}
    for name in _INS:
        a = _np.ascontiguousarray(inputs[name])
        arrays[f"in_{name}_dram"] = a
        args[name] = nc.dram_tensor(f"in_{name}_dram", a.shape, _mybir.dt.from_np(a.dtype),
                                    kind="ExternalInput").ap()
    shape = inputs["L0_attn_x"].shape
    out = nc.dram_tensor("out_0_dram", shape, _mybir.dt.float32, kind="ExternalOutput").ap()
    macaron_kernel(nc, args, out)
    r = _run(nc, [arrays], core_ids=[0])
    return r.results[0]["out_0_dram"]
```

```python
from contextlib import ExitStack

import concourse.bass as bass
from concourse import mybir

ALU = mybir.AluOpType
ACT = mybir.ActivationFunctionType
AX = mybir.AxisListType
F32 = mybir.dt.float32
BF16 = mybir.dt.bfloat16
I32 = mybir.dt.int32

P = 128
EPS = 1e-5
ROUND = 1.5 * 2 ** 23
LOWEST = -1e38


def macaron_kernel(nc, t_in, out):
    x_in = t_in["L0_attn_x"]
    NB, T, D = x_in.shape
    assert D == P and T % P == 0
    J = T // P
    WARM_UP = 16
    WARM = 6
    BG = NB // 2
    JD = J // 2
    NT = NB * J
    E, _, F2 = t_in["L0_ffn_gate_up_proj"].shape
    FM = F2 // 2
    FC = FM // P
    FS = t_in["L0_ffn_w_gate"].shape[0]
    SC = FS // P
    CF = t_in["L0_attn_cwk"].shape[1]
    CC = CF // P
    NBLK = NT + E - 1
    WMIX = ("k", "v", "r")

    ctx = ExitStack()
    with ctx:
        def sb(name, shape, dt=F32):
            return ctx.enter_context(nc.sbuf_tensor(name, shape, dt))

        def sem(name):
            return ctx.enter_context(nc.semaphore(name))

        bank = [ctx.enter_context(nc.psum_tensor(f"bank{i}", [P, 512], F32)) for i in range(8)]

        xs_dram = nc.dram_tensor("xs_dram", [NT * P, D], F32, kind="Internal").ap()
        SPARE = NT * P
        y_dram = nc.dram_tensor("y_dram", [SPARE + NBLK * P, D], F32, kind="Internal").ap()

        ROW = F2 + FC * D
        experts = sb("experts", [P, E * ROW])
        experts_e = experts[:, :].rearrange("p (e w) -> p e w", e=E)
        w_gate_raw = sb("w_gate_raw", [P, SC, D])
        w_up_raw = sb("w_up_raw", [P, SC, D])
        w_down_raw = sb("w_down_raw", [P, FS])
        w_router_raw = sb("w_router_raw", [E, D])
        w_gateT = sb("w_gateT", [P, SC, P])
        w_upT = sb("w_upT", [P, SC, P])
        w_downT = sb("w_downT", [P, SC, D])
        w_routerT = sb("w_routerT", [P, E])
        w_tm = {m: sb(f"w{m}", [P, D]) for m in WMIX}
        w_now = {m: sb(f"w{m}_now", [P, D]) for m in WMIX}
        w_prev = {m: sb(f"w{m}_prev", [P, D]) for m in WMIX}
        wo = sb("wo", [P, D])
        cwk = sb("cwk", [P, CF])
        cwr = sb("cwr", [P, D])
        cwv = sb("cwv", [P, CC, D])
        VEC = ["ln1_g", "ln1_b", "ln2_g", "ln2_b", "tm_mix_k", "tm_mix_v", "tm_mix_r",
               "time_decay", "time_first", "cm_mix_k", "cm_mix_r"]
        vec = {v: sb(v, [P, 1]) for v in VEC}
        one_minus = sb("one_minus", [P, 3])
        decay_exp = sb("decay_exp", [P, 1])
        decay = sb("decay", [P, 1])
        decay_row = sb("decay_row", [P, T])
        ident = sb("ident", [P, P])
        before = sb("before", [P, P], BF16)
        ones = sb("ones", [P, P], BF16)
        rank = sb("rank", [P, E])
        carry = sb("carry", [P, E, NT])
        block_no = sb("block_no", [P, NBLK])
        position_no = sb("position_no", [P, P])
        tile_no = sb("tile_no", [P, NT])
        row_no = sb("row_no", [P, 1])
        spare_row = sb("spare_row", [P, NBLK])
        half_neg = sb("half_neg", [P, 2 * NT])
        ones_row = sb("ones_row", [P, E])

        X = sb("X", [P, NT, D])
        xn = sb("xn", [P, NT, D])
        xs = sb("xs", [P, NT, D])
        xnT = sb("xnT", [P, NB, T])
        yg = xs
        stats = sb("stats", [P, NT, 6])
        mv = sb("mv", [P, NT, 2])
        veps = sb("veps", [P, NT])
        neg_mean = sb("neg_mean", [P, NT])
        rstd = sb("rstd", [P, NT])
        shift = sb("shift", [P, NT])
        best = sb("best", [P, NT])
        th_score = sb("th_score", [P, NT])
        score = sb("score", [P, NT])
        is_best = sb("is_best", [P, NT, E])
        ranked = sb("ranked", [P, NT, E])
        top_rank = sb("top_rank", [P, NT])
        onehot = sb("onehot", [P, NT, E], BF16)
        count = sb("count", [P, E])
        blocks_f = sb("blocks_f", [P, E])
        blocks = sb("blocks", [P, E])
        block_end = sb("block_end", [P, E + 1])
        steps = sb("steps", [P, E, NT])
        tile_start = sb("tile_start", [P, E, NT])
        slot_all = sb("slot_all", [P, NT, E])
        slot_sel = sb("slot_sel", [P, NT, E])
        slot_f = sb("slot_f", [P, NT])
        slot_block_r = sb("slot_block_r", [P, NT])
        slot_block = sb("slot_block", [P, NT])
        slot_pos = sb("slot_pos", [P, NT])
        kk_01 = sb("kk_01", [P, 2 * T])
        pos_hot = kk_01[:, :].bitcast(BF16).rearrange("p (t q) -> p t q", q=P)
        block_hot = sb("block_hot", [P, NT, NBLK], BF16)
        token_parts = sb("token_parts", [P, NT, 2, NBLK], BF16)
        token_low = sb("token_low", [P, NBLK])
        token_1 = sb("token_1", [P, NBLK])
        to_spare = sb("to_spare", [P, NBLK])
        row_from = sb("row_from", [P, NBLK], I32)
        row_to = sb("row_to", [P, NBLK], I32)
        past = sb("past", [1, NBLK, E - 1])
        block_expert_f = sb("block_expert_f", [1, NBLK])
        block_row = sb("block_row", [1, NBLK], I32)
        sg = [sb(f"sg{c}", [P, T]) for c in range(SC)]
        act = [sb(f"act{c}", [P, T]) for c in range(SC)]
        NXB = 8
        NYB = 4
        xb_all = sb("xb_all", [P, NXB, D])
        xb = [xb_all[:, i, :] for i in range(NXB)]
        xbT = [sb(f"xbT{i}", [P, P]) for i in range(2)]
        mg = [sb(f"mg{i}", [P, FM]) for i in range(2)]
        ma = [sb(f"ma{i}", [P, FM]) for i in range(2)]
        maT = [sb(f"maT{i}", [P, FC, P]) for i in range(2)]
        yb = [sb(f"yb{i}", [P, D]) for i in range(NYB)]

        def tiles(ap, b):
            return ap[:, J * b:J * b + J, :]

        def flat(ap, b):
            return ap[:, J * b:J * b + J, :].rearrange("p t d -> p (t d)")

        def two(name, shape):
            return [sb(f"{name}{i}", shape) for i in range(2)]

        a_stats = two("a_stats", [P, J, 6])
        a_mv = two("a_mv", [P, J, 2])
        a_veps = two("a_veps", [P, 2 * J])
        a_rstd = two("a_rstd", [P, 2 * J])
        h1 = [tiles(xn, i) for i in range(2)]
        a_in = [tiles(xn, 2 + i) for i in range(2)]
        x2 = [xnT[:, i, :].rearrange("p (t d) -> p t d", d=D) for i in range(2)]
        h2 = [xnT[:, 2 + i, :].rearrange("p (t d) -> p t d", d=D) for i in range(2)]
        dh = sg
        kk = [kk_01[:, 0:T], kk_01[:, T:2 * T], act[0], act[1]]
        h1T = two("h1T", [P, T + 1])
        peak = two("peak", [P, T + 1])
        d_now = two("d_now", [P, T])
        d_old = two("d_old", [P, T])
        d_out = two("d_out", [P, T])
        d_neg = two("d_neg", [P, T])
        d_pos = d_out
        e2b, e1b, e2, e1 = d_now, d_old, d_neg, d_pos
        kv = two("kv", [P, T])
        aa = two("aa", [P, T + 1])
        bb = two("bb", [P, T + 1])
        num_new = two("num_new", [P, T])
        num_old = two("num_old", [P, T])
        den_old = two("den_old", [P, T])
        th_r = two("th_r", [P, T])
        up = kv
        rw = num_new
        c_stats = two("c_stats", [P, J, 6])
        c_mv = two("c_mv", [P, J, 2])
        c_veps = two("c_veps", [P, J])
        c_rstd = two("c_rstd", [P, J])
        h2T = two("h2T", [P, T + 1])
        mix_k = two("mix_k", [P, T])
        mix_r = two("mix_r", [P, T])
        th_rr = [tiles(xb_all, i).rearrange("p t d -> p (t d)") for i in range(2)]

        s_x = [sem(f"s_xin{b}") for b in range(NB)]
        s_wsh = sem("s_wsh")
        s_wmoe = sem("s_wmoe")
        s_watt = sem("s_watt")
        s_cmem = sem("s_cmem")
        s_const = sem("s_const")
        s_wtp = sem("s_wtp")
        s_wt = sem("s_wt")
        s_stats = sem("s_stats")
        s_mv = sem("s_mv")
        s_veps = sem("s_veps")
        s_rstd = sem("s_rstd")
        s_shift = sem("s_shift")
        s_xn_d = sem("s_xn_d")
        s_xn_a = sem("s_xn_a")
        s_xnTp = sem("s_xnTp")
        s_xnT = sem("s_xnT")
        s_logit = sem("s_logit")
        s_best = sem("s_best")
        s_thsc = sem("s_thsc")
        s_score = sem("s_score")
        s_xs = sem("s_xs")
        s_rt = sem("s_rt")
        s_onehot = sem("s_onehot")
        s_count = sem("s_count")
        s_place = sem("s_place")
        s_pos_hot = sem("s_pos_hot")
        s_token = sem("s_token")
        s_rows = sem("s_rows")
        s_bexp = sem("s_bexp")
        s_xst = sem("s_xst")
        s_sgu = sem("s_sgu")
        s_ssilu = sem("s_ssilu")
        s_up = sem("s_up")
        s_sact = sem("s_sact")
        s_sdn = sem("s_sdn")
        s_sres = sem("s_sres")
        s_xb = [sem(f"s_xb{i}") for i in range(NXB)]
        s_xbTp = sem("s_xbTp")
        s_xbT = sem("s_xbT")
        s_mgu = sem("s_mgu")
        s_mg = sem("s_mg")
        s_ma = sem("s_ma")
        s_maTp = sem("s_maTp")
        s_maT = sem("s_maT")
        s_my = sem("s_my")
        s_yb = sem("s_yb")
        s_yst = [sem(f"s_yst{i}") for i in range(NYB)]
        s_yg = [sem(f"s_yg{b}") for b in range(NB)]
        s_x1 = sem("s_x1")
        s_out = sem("s_out")

        ATT = ["a_stats", "a_mv", "a_veps", "a_rstd", "a_norm", "h1Tp", "h1T", "k", "v", "r", "th_r", "peak",
               "d_now", "d_out", "d_old", "d_neg", "d_pos", "e2b", "e1b", "e2", "e1", "kv", "aa", "bb",
               "num_new", "num_old", "den_old", "den", "num", "rden", "wkv", "rw", "wo", "x2", "c_stats",
               "c_mv", "c_veps", "c_rstd", "h2", "h2Tp", "h2T", "dh", "mix_k", "mix_r", "cwk", "pos_kk",
               "kk", "a_in", "rr", "th_rr", "cwv", "x12", "rcv", "x_att"]
        sa = {n: sem("s_" + n + "_a") for n in ATT}
        s_edge = sem("s_edge")
        s_omix = sem("s_omix")
        s_wmix = sem("s_wmix")
        s_dexp = sem("s_dexp")
        s_prep = sem("s_prep")

        def pipelined(steps):
            for j in range(NB + max(lag for _, lag in steps)):
                for step, lag in steps:
                    if 0 <= j - lag < NB:
                        step(j - lag)

        x_dram = x_in.rearrange("b (t p) d -> b p t d", p=P)
        out_dram = out.rearrange("b (t p) d -> b p t d", p=P)

        block = ctx.enter_context(nc.Block())

        @block.sync
        def _(sp):
            for b in range(NB):
                sp.dma_start(tiles(X, b), x_dram[b]).then_inc(s_x[b], 16)
                if b == 0:
                    sp.dma_start(w_router_raw[:, :], t_in["L0_ffn_w_router"]).then_inc(s_wsh, 16)
                    sp.dma_start(w_gate_raw[:, :, :], t_in["L0_ffn_w_gate"].rearrange(
                        "(c p) d -> p c d", p=P)).then_inc(s_wsh, 16)
                    sp.dma_start(w_up_raw[:, :, :], t_in["L0_ffn_w_up"].rearrange(
                        "(c p) d -> p c d", p=P)).then_inc(s_wsh, 16)
                    sp.dma_start(w_down_raw[:, :], t_in["L0_ffn_w_down"]).then_inc(s_wsh, 16)
            def rows_dram(dram, b):
                return dram[b * T:b * T + T, :].rearrange("(t p) d -> p t d", p=P)

            for e in range(0, E, 4):
                sp.dma_start(experts_e[:, e:e + 4, 0:F2], t_in["L0_ffn_gate_up_proj"][e:e + 4].rearrange(
                    "e h f -> h e f")).then_inc(s_wmoe, 16)
                for i in range(e, e + 4):
                    sp.dma_start(experts_e[:, i, F2:ROW].rearrange("p (c d) -> p c d", c=FC),
                                 t_in["L0_ffn_down_proj"][i].rearrange("(c p) d -> p c d", p=P)
                                 ).then_inc(s_wmoe, 16)
            def load_weights():
                for v in VEC:
                    sp.dma_start(vec[v][:, :], t_in["L0_attn_" + v].rearrange("(p a) -> p a", a=1)
                                 ).then_inc(s_watt, 16)
                for m in WMIX:
                    sp.dma_start(w_tm[m][:, :], t_in["L0_attn_w" + m]).then_inc(s_watt, 16)
                sp.dma_start(wo[:, :], t_in["L0_attn_wo"]).then_inc(s_watt, 16)
                sp.dma_start(cwk[:, :], t_in["L0_attn_cwk"]).then_inc(s_watt, 16)
                sp.dma_start(cwr[:, :], t_in["L0_attn_cwr"]).then_inc(s_watt, 16)
                sp.dma_start(cwv[:, :, :], t_in["L0_attn_cwv"].rearrange("(c p) d -> p c d", p=P)
                             ).then_inc(s_watt, 16)

            def store_tokens(v):
                if v:
                    for k in range(NXB):
                        sp.wait_ge(s_xb[k], 16 * len([i for i in range(NBLK) if i % NXB == k]))
                for b in range(NB):
                    sp.wait_ge(s_xs, v * NB + b + 1)
                    sp.dma_start(rows_dram(xs_dram, b), tiles(xs, b)).then_inc(s_xst, 16)

            def load_outputs(v):
                for k in range(NYB):
                    sp.wait_ge(s_yst[k], 16 * len([i for i in range((v + 1) * NBLK) if i % NYB == k]))
                sp.wait_ge(s_xst, 16 * NB * (v + 1))
                for b in range(NB):
                    sp.dma_start(tiles(yg, b), rows_dram(y_dram, b)).then_inc(s_yg[b], 16)

            store_tokens(0)
            load_weights()
            load_outputs(0)
            store_tokens(1)
            load_outputs(1)
            for b in range(NB):
                sp.wait_ge(s_x1, NB + b + 1)
                sp.dma_start(out_dram[b], tiles(X, b)).then_inc(s_out, 16)
            sp.wait_ge(s_out, 16 * NB)

        @block.gpsimd
        def _(g):
            g.memset(ident[:, :], 0.0).then_inc(s_cmem, 1)
            g.memset(before[:, :], 1.0).then_inc(s_cmem, 1)
            g.memset(carry[:, :, :], 1.0).then_inc(s_cmem, 1)
            g.memset(ones[:, :], 1.0).then_inc(s_const, 1)
            g.memset(half_neg[:, :], -0.5).then_inc(s_const, 1)
            g.memset(ones_row[:, :], 1.0).then_inc(s_const, 1)
            g.memset(block_end[:, :], 0.0).then_inc(s_const, 1)
            g.iota(rank[:, :], pattern=[[-1, E]], base=E, channel_multiplier=0,
                   allow_small_or_imprecise_dtypes=True).then_inc(s_const, 1)
            def count_up(out_, step, base, channel):
                g.iota(out_[:, :], pattern=[[step, out_.shape[1]]], base=base, channel_multiplier=channel,
                       allow_small_or_imprecise_dtypes=True).then_inc(s_const, 1)

            count_up(block_no, 1, 0, 0)
            count_up(position_no, 1, 0, 0)
            count_up(tile_no, 1, 0, 0)
            count_up(row_no, 0, 1, 1)
            count_up(spare_row, P, SPARE + 1, 1)
            g.wait_ge(s_cmem, 3)
            g.affine_select(out=ident[:, :], in_=ident[:, :], compare_op=ALU.not_equal, fill=1.0,
                            base=0, pattern=[[-1, P]], channel_multiplier=1).then_inc(s_const, 1)
            g.affine_select(out=before[:, :], in_=before[:, :], compare_op=ALU.is_gt, fill=0.0,
                            base=0, pattern=[[1, P]], channel_multiplier=-1).then_inc(s_const, 1)
            g.affine_select(out=carry[:, :, :], in_=carry[:, :, :], compare_op=ALU.is_gt, fill=0.0,
                            base=0, pattern=[[0, E], [1, NT]], channel_multiplier=0
                            ).then_inc(s_const, 1)

            def rstd_ffn(v, b):
                n, tiles_b = v * NB + b + 1, slice(J * b, J * b + J)
                g.wait_ge(s_mv, n)
                g.tensor_scalar(neg_mean[:, tiles_b], mv[:, tiles_b, 0], -1.0, None, ALU.mult)
                g.tensor_scalar(veps[:, tiles_b], mv[:, tiles_b, 1], EPS, None, ALU.add).then_inc(s_veps, 1)
                g.wait_ge(s_veps, n)
                g.tensor_tensor(rstd[:, tiles_b], veps[:, tiles_b], half_neg[:, 0:J], ALU.pow
                                ).then_inc(s_rstd, 1)
                g.wait_ge(s_rstd, n)
                g.tensor_tensor(shift[:, tiles_b], neg_mean[:, tiles_b], rstd[:, tiles_b], ALU.mult
                                ).then_inc(s_shift, 1)

            def act_chunk(v, b, c):
                n = (v * NB + b) * SC + c
                g.wait_ge(s_ssilu, n + 1)
                if n >= SC:
                    g.wait_ge(s_sdn, v * NB + b)
                    g.wait_ge(s_sact, n)
                g.wait_ge(s_up, (v * BG + b) * SC + c + 1)
                g.tensor_tensor(act[c][:, :], sg[c][:, :], up[c][:, :], ALU.mult
                                ).then_inc(s_sact, 1)

            def first_acts(v):
                for b in range(BG):
                    for c in range(SC):
                        act_chunk(v, b, c)

            def move_blocks(v):
                o = v * NBLK

                def gather(i):
                    n = o + i
                    if n >= NXB:
                        g.wait_ge(s_xbTp, n - NXB + 1)
                    g.indirect_dma_start(
                        out=xb[n % NXB], out_offset=None, in_=xs_dram,
                        in_offset=bass.IndirectOffsetOnAxis(ap=row_from[:, i:i + 1], axis=0)
                    ).then_inc(s_xb[n % NXB], 16)

                def scatter(i):
                    n = o + i
                    g.wait_ge(s_yb, n + 1)
                    g.indirect_dma_start(
                        out=y_dram, out_offset=bass.IndirectOffsetOnAxis(ap=row_to[:, i:i + 1], axis=0),
                        in_=yb[n % NYB][:, :], in_offset=None).then_inc(s_yst[n % NYB], 16)

                if v:
                    for b in range(NB):
                        g.wait_ge(s_yg[b], 16 * v)
                g.wait_ge(s_xst, 16 * NB * (v + 1))
                g.wait_ge(s_rows, 3 * (v + 1))
                AHEAD = NXB + 2
                for i in range(NBLK + AHEAD):
                    if i < NBLK:
                        gather(i)
                    if i >= AHEAD:
                        scatter(i - AHEAD)

            def rwkv():
                def rstd_in(b):
                    i, n = b % 2, b + 1
                    g.wait_ge(sa["a_mv"], n)
                    g.tensor_scalar(a_veps[i][:, 0:J], a_mv[i][:, :, 1], EPS, None, ALU.add)
                    g.tensor_scalar(a_veps[i][:, J:2 * J], a_mv[i][:, :, 1], 1.0 + EPS, EPS * EPS,
                                    ALU.mult, ALU.add).then_inc(sa["a_veps"], 1)
                    g.wait_ge(sa["a_veps"], n)
                    if b >= 2:
                        g.wait_ge(sa["a_norm"], b - 1)
                    g.tensor_tensor(a_rstd[i][:, :], a_veps[i][:, :], half_neg[:, 0:2 * J], ALU.pow
                                    ).then_inc(sa["a_rstd"], 1)

                def rstd_mid(b):
                    i, n = b % 2, b + 1
                    g.wait_ge(sa["c_mv"], n)
                    g.tensor_scalar(c_veps[i][:, :], c_mv[i][:, :, 1], EPS, None, ALU.add
                                    ).then_inc(sa["c_veps"], 1)
                    g.wait_ge(sa["c_veps"], n)
                    if b >= 2:
                        g.wait_ge(sa["h2"], b - 1)
                    g.tensor_tensor(c_rstd[i][:, :], c_veps[i][:, :], half_neg[:, 0:J], ALU.pow
                                    ).then_inc(sa["c_rstd"], 1)

                def fall(b):
                    i, n = b % 2, b + 1
                    g.wait_ge(sa["peak"], n)
                    if b >= 2:
                        g.wait_ge(sa["aa"], b - 1)
                        g.wait_ge(sa["bb"], b - 1)
                    g.tensor_tensor(d_old[i][:, :], peak[i][:, 0:T], peak[i][:, 1:T + 1], ALU.subtract
                                    ).then_inc(sa["d_old"], 1)

                def block_input(b):
                    i, n = b % 2, b + 1
                    g.wait_ge(sa["a_rstd"], n)
                    if b >= 2:
                        g.wait_ge(sa["x2"], b - 1)
                    for j in range(J):
                        m = g.tensor_scalar(a_in[i][:, j, :], X[:, J * b + j, :], a_mv[i][:, j, 0:1],
                                            a_rstd[i][:, j:j + 1], ALU.subtract, ALU.mult)
                    m.then_inc(sa["a_in"], 1)

                def change(b):
                    i, n = b % 2, b + 1
                    g.wait_ge(sa["h2T"], n)
                    if b >= 2:
                        g.wait_ge(sa["mix_k"], b - 1)
                        g.wait_ge(sa["mix_r"], b - 1)
                    g.tensor_tensor(dh[i][:, :], h2T[i][:, 1:T + 1], h2T[i][:, 0:T], ALU.subtract
                                    ).then_inc(sa["dh"], 1)

                def old_numerator(b):
                    i, n = b % 2, b + 1
                    g.wait_ge(sa["e1"], n)
                    g.wait_ge(sa["aa"], n)
                    if b >= 2:
                        g.wait_ge(sa["num"], b - 1)
                    g.tensor_tensor(num_old[i][:, :], e1[i][:, :], aa[i][:, 0:T], ALU.mult
                                    ).then_inc(sa["num_old"], 1)

                def old_denominator(b):
                    i, n = b % 2, b + 1
                    g.wait_ge(sa["e1"], n)
                    g.wait_ge(sa["bb"], n)
                    if b >= 2:
                        g.wait_ge(sa["wkv"], b - 1)
                    g.tensor_tensor(den_old[i][:, :], e1[i][:, :], bb[i][:, 0:T], ALU.mult
                                    ).then_inc(sa["den_old"], 1)

                def denominator(b):
                    i, n = b % 2, b + 1
                    g.wait_ge(sa["den_old"], n)
                    g.wait_ge(sa["e2"], n)
                    g.tensor_tensor(den_old[i][:, :], den_old[i][:, :], e2[i][:, :], ALU.add
                                    ).then_inc(sa["den"], 1)

                def two_inputs(b):
                    i, n = b % 2, b + 1
                    g.wait_ge(sa["x2"], n)
                    g.wait_ge(sa["a_in"], n)
                    g.tensor_tensor(flat(X, b), flat(X, b), x2[i][:, :, :].rearrange("p t d -> p (t d)"),
                                    ALU.add).then_inc(sa["x12"], 1)

                def rstd_out(b):
                    rstd_ffn(1, b)

                pipelined([(two_inputs, 3), (rstd_in, 0), (fall, 1), (change, 3), (block_input, 1),
                           (old_denominator, 1), (old_numerator, 1), (denominator, 1), (rstd_mid, 2),
                           (rstd_out, 6)])

            for i in range(2):
                g.memset(h1T[i][:, 0:1], 0.0)
                g.memset(h2T[i][:, 0:1], 0.0)
                g.memset(aa[i][:, 0:1], 0.0)
                g.memset(bb[i][:, 0:1], 0.0)
                last = g.memset(peak[i][:, 0:1], LOWEST)
            last.then_inc(s_edge, 1)
            for b in range(NB):
                rstd_ffn(0, b)
            first_acts(0)
            move_blocks(0)
            rwkv()
            first_acts(1)
            move_blocks(1)

        @block.scalar
        def _(a):
            a.wait_ge(s_wtp, 1)
            a.copy(w_gateT[:, :, :].rearrange("p c f -> p (c f)"), bank[2][:, 0:FS])
            a.copy(w_upT[:, :, :].rearrange("p c f -> p (c f)"), bank[3][:, 0:FS])
            a.copy(w_downT[:, :, :].rearrange("p c d -> p (c d)"), bank[4][:, 0:SC * D])
            a.copy(w_routerT[:, :], bank[5][:, 0:E]).then_inc(s_wt, 1)

            def normalize(v, b):
                a.wait_ge(s_shift, v * NB + b + 1)
                if v and b < 2:
                    a.wait_ge(sa["h1Tp"], b + 3)
                if v and b >= 2:
                    a.wait_ge(sa["x2"], b + 1)
                for t in range(J * b + JD, J * b + J):
                    i = a.activation(xn[:, t, :], X[:, t, :], ACT.Identity, scale=rstd[:, t:t + 1],
                                     bias=shift[:, t:t + 1])
                i.then_inc(s_xn_a, 1)

            def turned(v, b):
                a.wait_ge(s_xnTp, v * NB + b + 1)
                if v and b < 2:
                    a.wait_ge(sa["x12"], b + 3)
                    a.wait_ge(sa["h2"], b + 3)
                if v and b >= 2:
                    a.wait_ge(sa["h2Tp"], b + 1)
                a.copy(xnT[:, b, :], bank[1 if v else b % 2][:, :]).then_inc(s_xnT, 1)

            def ffn_front(v):
                def silu(b, c):
                    n = (v * NB + b) * SC + c
                    a.wait_ge(s_sgu, n + 1)
                    if n >= SC:
                        a.wait_ge(s_sact, n + 1 - SC)
                    a.activation(sg[c][:, :], bank[2 + 2 * c][:, :], ACT.Silu).then_inc(s_ssilu, 1)
                    if b < BG:
                        a.copy(up[c][:, :], bank[3 + 2 * c][:, :]).then_inc(s_up, 1)

                def scale(b):
                    if b == 0:
                        a.wait_ge(s_score, v + 1)
                        if v:
                            a.wait_ge(s_x1, NB)
                    for t in range(J * b, J * b + J):
                        i = a.activation(xs[:, t, :], xn[:, t, :], ACT.Copy, scale=score[:, t:t + 1])
                    i.then_inc(s_xs, 1)

                if v == 0:
                    normalize(0, 0)
                    for b in range(NB):
                        if b + 1 < NB:
                            normalize(0, b + 1)
                        turned(0, b)
                a.wait_ge(s_best, v + 1)
                a.activation(th_score[:, :], best[:, :], ACT.Tanh, scale=0.5).then_inc(s_thsc, 1)
                silu(0, 0)
                scale(0)
                scale(1)
                silu(0, 1)
                scale(2)
                silu(1, 0)
                scale(3)
                silu(1, 1)
                for b in range(BG, NB):
                    for c in range(SC):
                        silu(b, c)

            def moe(v):
                def silu(i, k):
                    n = v * NBLK + i
                    a.wait_ge(s_mgu, n + 1)
                    a.activation(mg[k % 2][:, :], bank[2 + k % 2][:, 0:FM], ACT.Silu).then_inc(s_mg, 1)

                def turn(i, k):
                    n = v * NBLK + i
                    a.wait_ge(s_maTp, n + 1)
                    a.copy(maT[k % 2][:, :, :].rearrange("p c f -> p (c f)"),
                           bank[4 + k % 2][:, 0:FM]).then_inc(s_maT, 1)

                o = v * NBLK
                silu(0, o)
                loops = (NBLK - 1) // NYB
                with a.Fori(0, loops) as r:
                    for k in range(NYB):
                        i = r * NYB + (1 + k)
                        silu(i, o + 1 + k)
                        turn(i - 1, o + k)
                for i in range(1 + loops * NYB, NBLK + 1):
                    if i < NBLK:
                        silu(i, o + i)
                    turn(i - 1, o + i - 1)

            def rwkv():
                def exp_row(b, name, out_, in_, scale=1.0, bias=0.0):
                    a.activation(out_[b % 2][:, :], in_[b % 2][:, :], ACT.Exp, scale=scale, bias=bias
                                 ).then_inc(sa[name], 1)

                def turned_in(b):
                    i, n = b % 2, b + 1
                    a.wait_ge(sa["h1Tp"], n)
                    if b == 0:
                        a.wait_ge(s_edge, 1)
                    if b >= 2:
                        for m in WMIX:
                            a.wait_ge(sa[m], b - 1)
                    a.activation(h1T[i][:, 1:T + 1], bank[0][:, :], ACT.Identity,
                                 scale=vec["ln1_g"][:, 0:1], bias=vec["ln1_b"][:, 0:1]
                                 ).then_inc(sa["h1T"], 1)

                def turned_mid(b):
                    i, n = b % 2, b + 1
                    a.wait_ge(sa["h2Tp"], n)
                    if b >= 2:
                        a.wait_ge(sa["mix_k"], b - 1)
                        a.wait_ge(sa["mix_r"], b - 1)
                    a.activation(h2T[i][:, 1:T + 1], bank[0][:, :], ACT.Identity,
                                 scale=vec["ln2_g"][:, 0:1], bias=vec["ln2_b"][:, 0:1]
                                 ).then_inc(sa["h2T"], 1)

                def exp_now(b):
                    a.wait_ge(sa["d_now"], b + 1)
                    exp_row(b, "e2b", e2b, d_now)

                def exp_old(b):
                    a.wait_ge(sa["d_old"], b + 1)
                    if b == 0:
                        a.wait_ge(s_prep, 1)
                    exp_row(b, "e1b", e1b, d_old, bias=decay[:, 0:1])

                def two_sides(b):
                    i, n = b % 2, b + 1
                    a.wait_ge(sa["d_out"], n)
                    if b >= 2:
                        a.wait_ge(sa["den"], b - 1)
                        a.wait_ge(sa["num_new"], b - 1)
                    a.activation(d_neg[i][:, :], d_out[i][:, :], ACT.Relu, scale=-1.0).then_inc(sa["d_neg"], 1)
                    a.wait_ge(sa["d_neg"], n)
                    a.activation(d_pos[i][:, :], d_out[i][:, :], ACT.Relu).then_inc(sa["d_pos"], 1)

                def exp_new_out(b):
                    a.wait_ge(sa["d_neg"], b + 1)
                    exp_row(b, "e2", e2, d_neg, scale=-1.0)

                def exp_old_out(b):
                    a.wait_ge(sa["d_pos"], b + 1)
                    exp_row(b, "e1", e1, d_pos, scale=-1.0)

                def receptance(b):
                    a.wait_ge(sa["r"], b + 1)
                    if b >= 2:
                        a.wait_ge(sa["rw"], b - 1)
                    a.activation(th_r[b % 2][:, :], bank[3][:, :], ACT.Tanh, scale=0.5
                                 ).then_inc(sa["th_r"], 1)

                def squared_relus(b, c0):
                    for c in range(c0, c0 + 2):
                        a.wait_ge(sa["cwk"], CC * b + c + 1)
                        if b >= 1:
                            a.wait_ge(sa["cwv"], b)
                        a.activation(kk[c][:, :], bank[6 + c % 2][:, :], ACT.Relu
                                     ).then_inc(sa["pos_kk"], 1)
                    for c in range(c0, c0 + 2):
                        a.wait_ge(sa["pos_kk"], CC * b + c + 1)
                        a.activation(kk[c][:, :], kk[c][:, :], ACT.Square).then_inc(sa["kk"], 1)

                def first_relus(b):
                    squared_relus(b, 0)

                def last_relus(b):
                    squared_relus(b, 2)

                def gate(b):
                    a.wait_ge(sa["rr"], b + 1)
                    if b >= 2:
                        a.wait_ge(sa["rcv"], b - 1)
                    a.activation(th_rr[b % 2], bank[4][:, :], ACT.Tanh, scale=0.5
                                 ).then_inc(sa["th_rr"], 1)

                def normalize_out(b):
                    normalize(1, b)

                def turned_out(b):
                    turned(1, b)

                pipelined([(exp_old, 1), (turned_in, 0), (exp_old_out, 1), (turned_out, 7),
                           (receptance, 1), (first_relus, 3), (last_relus, 3), (gate, 3),
                           (normalize_out, 6), (two_sides, 0), (exp_new_out, 0), (turned_mid, 2),
                           (exp_now, 0)])

            ffn_front(0)
            moe(0)
            a.wait_ge(s_watt, 16 * (len(VEC) + 7))
            a.activation(decay_exp[:, :], vec["time_decay"][:, :], ACT.Exp).then_inc(s_dexp, 1)
            rwkv()
            ffn_front(1)
            moe(1)

        @block.vector
        def _(d):
            def norm_ffn(v, b):
                n = v * NB + b + 1
                if v == 0:
                    d.wait_ge(s_x[b], 16)
                else:
                    d.wait_ge(sa["x_att"], b + 1)
                for t in range(J * b, J * b + J):
                    i = d.bn_stats(stats[:, t, :], X[:, t, :])
                i.then_inc(s_stats, 1)
                d.wait_ge(s_stats, n)
                for t in range(J * b, J * b + J):
                    i = d.bn_aggr(mv[:, t, :], stats[:, t, :])
                i.then_inc(s_mv, 1)

            def scale_ffn(v, b):
                d.wait_ge(s_rstd, v * NB + b + 1)
                if v and b < 2:
                    d.wait_ge(sa["h1Tp"], b + 3)
                for t in range(J * b, J * b + JD):
                    i = d.tensor_scalar(xn[:, t, :], X[:, t, :], mv[:, t, 0:1], rstd[:, t:t + 1],
                                        ALU.subtract, ALU.mult)
                i.then_inc(s_xn_d, 1)

            def route(v):
                c = [v * 16]

                def done(ins):
                    c[0] += 1
                    ins.then_inc(s_rt, 1)
                    d.wait_ge(s_rt, c[0])

                logit = bank[7][:, 0:NT * E].rearrange("p (t e) -> p t e", e=E)
                d.wait_ge(s_logit, v * NB + NB)
                d.tensor_reduce(best[:, :], logit, AX.X, ALU.max).then_inc(s_best, 1)
                d.wait_ge(s_best, v + 1)
                done(d.tensor_tensor(is_best[:, :, :], logit,
                                     best[:, :].unsqueeze(2).to_broadcast([P, NT, E]), ALU.is_ge))
                done(d.tensor_tensor(ranked[:, :, :], is_best[:, :, :],
                                     rank[:, :].unsqueeze(1).to_broadcast([P, NT, E]), ALU.mult))
                done(d.tensor_reduce(top_rank[:, :], ranked[:, :, :], AX.X, ALU.max))
                d.tensor_tensor(onehot[:, :, :], rank[:, :].unsqueeze(1).to_broadcast([P, NT, E]),
                                top_rank[:, :].unsqueeze(2).to_broadcast([P, NT, E]),
                                ALU.is_equal).then_inc(s_onehot, 1)
                d.wait_ge(s_thsc, v + 1)
                d.tensor_scalar(score[:, :], th_score[:, :], 1.0, 0.5, ALU.add, ALU.mult
                                ).then_inc(s_score, 1)
                total = bank[0][:, 0:NT * E].rearrange("p (t e) -> p e t", e=E)
                d.wait_ge(s_count, v + 1)
                done(d.tensor_reduce(count[:, :], total, AX.X, ALU.add))
                done(d.tensor_scalar(blocks_f[:, :], count[:, :], (P - 1) / 2.0, 1.0 / P, ALU.add,
                                     ALU.mult))
                done(d.tensor_scalar(blocks[:, :], blocks_f[:, :], ROUND, -ROUND, ALU.add, ALU.add))
                done(d.tensor_tensor_scan(block_end[:, 1:E + 1], ones_row[:, :], blocks[:, :], 0.0,
                                          ALU.mult, ALU.add))
                d.tensor_copy(steps[:, :, 1:NT], total[:, :, 0:NT - 1])
                done(d.tensor_scalar(steps[:, :, 0], block_end[:, 0:E], float(P), None, ALU.mult))
                done(d.tensor_tensor_scan(tile_start[:, :, :].rearrange("p e t -> p (e t)"),
                                          carry[:, :, :].rearrange("p e t -> p (e t)"),
                                          steps[:, :, :].rearrange("p e t -> p (e t)"), 0.0,
                                          ALU.mult, ALU.add))
                done(d.tensor_tensor(slot_all[:, :, :],
                                     tile_start[:, :, :].rearrange("p e t -> p t e"),
                                     bank[1][:, 0:NT * E].rearrange("p (t e) -> p t e", e=E), ALU.add))
                done(d.tensor_tensor(slot_sel[:, :, :], slot_all[:, :, :], onehot[:, :, :], ALU.mult))
                done(d.tensor_reduce(slot_f[:, :], slot_sel[:, :, :], AX.X, ALU.add))
                done(d.tensor_scalar(slot_block_r[:, :], slot_f[:, :], -(P - 1) / 2.0, 1.0 / P, ALU.add,
                                     ALU.mult))
                done(d.tensor_scalar(slot_block[:, :], slot_block_r[:, :], ROUND, -ROUND, ALU.add, ALU.add))
                done(d.scalar_tensor_tensor(out=slot_pos[:, :], in0=slot_block[:, :], scalar=-float(P),
                                            in1=slot_f[:, :], op0=ALU.mult, op1=ALU.add))
                d.tensor_tensor(block_hot[:, :, :], block_no[:, :].unsqueeze(1).to_broadcast([P, NT, NBLK]),
                                slot_block[:, :].unsqueeze(2).to_broadcast([P, NT, NBLK]),
                                ALU.is_equal).then_inc(s_place, 1)
                d.wait_ge(s_place, v + 1)
                d.tensor_tensor(token_parts[:, :, 0, :], block_hot[:, :, :],
                                tile_no[:, :].unsqueeze(2).to_broadcast([P, NT, NBLK]), ALU.mult)
                d.tensor_scalar(token_parts[:, :, 1, :], block_hot[:, :, :], row_no[:, 0:1], None, ALU.mult)
                if v:
                    d.wait_ge(sa["cwv"], NB)
                for t in range(NT):
                    i = d.tensor_scalar(pos_hot[:, t, :], position_no[:, :], slot_pos[:, t:t + 1], None,
                                        ALU.is_equal)
                    if t % J == J - 1:
                        i.then_inc(s_pos_hot, 1)
                assert c[0] == 16 * v + 15, c
                d.wait_ge(s_token, v + 1)
                tile_of, row_of = bank[7][:, 0:NBLK], bank[7][:, NBLK:2 * NBLK]
                d.tensor_scalar(token_low[:, :], row_of, 1.0, None, ALU.mult).then_inc(s_rows, 1)
                d.wait_ge(s_rows, 3 * v + 1)
                d.scalar_tensor_tensor(out=token_1[:, :], in0=tile_of, scalar=float(P),
                                       in1=token_low[:, :], op0=ALU.mult, op1=ALU.add).then_inc(s_rows, 1)
                d.wait_ge(s_rows, 3 * v + 2)
                d.tensor_scalar(row_from[:, :], token_1[:, :], -1.0, 0.0, ALU.add, ALU.max)
                d.scalar_tensor_tensor(out=to_spare[:, :], in0=token_1[:, :], scalar=0.0,
                                       in1=spare_row[:, :], op0=ALU.is_equal, op1=ALU.mult
                                       ).then_inc(s_rt, 1)
                d.wait_ge(s_rt, 16 * (v + 1))
                d.scalar_tensor_tensor(out=row_to[:, :], in0=token_1[:, :], scalar=-1.0,
                                       in1=to_spare[:, :], op0=ALU.add, op1=ALU.add).then_inc(s_rows, 1)
                d.tensor_tensor(past[:, :, :],
                                block_no[0:1, :].unsqueeze(2).to_broadcast([1, NBLK, E - 1]),
                                block_end[0:1, 1:E].unsqueeze(1).to_broadcast([1, NBLK, E - 1]),
                                ALU.is_ge).then_inc(s_bexp, 1)
                d.wait_ge(s_bexp, 3 * v + 1)
                d.tensor_reduce(block_expert_f[:, :], past[:, :, :], AX.X, ALU.add).then_inc(s_bexp, 1)
                d.wait_ge(s_bexp, 3 * v + 2)
                d.tensor_scalar(block_row[:, :], block_expert_f[:, :], float(ROW), None, ALU.mult
                                ).then_inc(s_bexp, 1)

            def act_chunk(v, b, c):
                n = (v * NB + b) * SC + c
                d.wait_ge(s_ssilu, n + 1)
                d.wait_ge(s_sact, n)
                if n >= SC:
                    d.wait_ge(s_sdn, v * NB + b)
                d.tensor_tensor(act[c][:, :], sg[c][:, :], bank[3 + 2 * c][:, :], ALU.mult
                                ).then_inc(s_sact, 1)

            def residual(v, b):
                d.wait_ge(s_sdn, v * NB + b + 1)
                d.scalar_tensor_tensor(out=flat(X, b), in0=bank[6][:, :], scalar=0.5,
                                       in1=flat(X, b), op0=ALU.mult, op1=ALU.add
                                       ).then_inc(s_sres, 1)

            def moe(v):
                def xT(i, k):
                    n = v * NBLK + i
                    d.wait_ge(s_xbTp, n + 1)
                    d.tensor_copy(xbT[k % 2][:, :], bank[k % 2][:, 0:P]
                                  ).then_inc(s_xbT, 1)

                def gate(i, k):
                    n = v * NBLK + i
                    d.wait_ge(s_mg, n + 1)
                    d.tensor_tensor(ma[k % 2][:, :], mg[k % 2][:, :], bank[2 + k % 2][:, FM:2 * FM],
                                    ALU.mult).then_inc(s_ma, 1)

                def y(i, k):
                    n = v * NBLK + i
                    d.wait_ge(s_my, n + 1)
                    if n >= NYB:
                        d.wait_ge(s_yst[k % NYB], 16 * (n // NYB))
                    d.tensor_scalar(yb[k % NYB][:, :], bank[6 + k % 2][:, 0:P], 0.5,
                                    None, ALU.mult).then_inc(s_yb, 1)

                o = v * NBLK
                def slot(i):
                    if i + 2 < NBLK:
                        xT(i + 2, o + i + 2)
                    if 0 <= i < NBLK:
                        gate(i, o + i)
                    if i >= 2:
                        y(i - 2, o + i - 2)

                first = NYB + 2
                loops = (NBLK - 2 - first) // NYB
                for i in range(-2, first):
                    slot(i)
                with d.Fori(0, loops) as r:
                    for k in range(NYB):
                        i = r * NYB + (first + k)
                        n = o + first + k
                        xT(i + 2, n + 2)
                        gate(i, n)
                        d.wait_ge(s_my, i + (o - 1))
                        d.wait_ge(s_yst[(n - 2) % NYB], r * 16 + 16 * ((n - 2) // NYB))
                        d.tensor_scalar(yb[(n - 2) % NYB][:, :], bank[6 + n % 2][:, 0:P], 0.5,
                                        None, ALU.mult).then_inc(s_yb, 1)
                for i in range(first + loops * NYB, NBLK + 2):
                    slot(i)

            def ffn(v):
                if v == 0:
                    for b in range(NB):
                        norm_ffn(v, b)
                        if b:
                            scale_ffn(v, b - 1)
                    scale_ffn(v, NB - 1)
                route(v)
                for b in range(BG - 1):
                    residual(v, b)
                for b in range(BG, NB):
                    act_chunk(v, b, 0)
                    residual(v, b - 1)
                    act_chunk(v, b, 1)
                residual(v, NB - 1)
                moe(v)

            def add_moe(v):
                for b in range(NB):
                    d.wait_ge(s_yg[b], 16 * (v + 1))
                    d.tensor_tensor(flat(X, b), flat(X, b), flat(yg, b), ALU.add).then_inc(s_x1, 1)

            def prepare():
                d.wait_ge(s_watt, 16 * (len(VEC) + 7))
                for j, m in enumerate(WMIX):
                    i = d.tensor_scalar(one_minus[:, j:j + 1], vec["tm_mix_" + m][:, :], -1.0, 1.0,
                                        ALU.mult, ALU.add)
                i.then_inc(s_omix, 1)
                d.wait_ge(s_omix, 1)
                for j, m in enumerate(WMIX):
                    d.tensor_scalar(w_now[m][:, :], w_tm[m][:, :], vec["tm_mix_" + m][:, 0:1], None, ALU.mult)
                    i = d.tensor_scalar(w_prev[m][:, :], w_tm[m][:, :], one_minus[:, j:j + 1], None, ALU.mult)
                i.then_inc(s_wmix, 1)
                d.wait_ge(s_dexp, 1)
                d.tensor_scalar(decay[:, :], decay_exp[:, :], -1.0, None, ALU.mult).then_inc(s_prep, 1)
                d.wait_ge(s_prep, 1)
                d.tensor_copy(decay_row[:, :], decay[:, 0:1].to_broadcast([P, T])).then_inc(s_prep, 1)
                d.wait_ge(s_prep, 2)

            def rwkv():
                def wait(name, n):
                    if n > 0:
                        d.wait_ge(sa[name], n)

                def inputs(b):
                    i, n = b % 2, b + 1
                    d.wait_ge(s_yg[b], 16)
                    d.tensor_tensor(flat(X, b), flat(X, b), flat(yg, b), ALU.add).then_inc(s_x1, 1)
                    d.wait_ge(s_x1, n)
                    for j in range(J):
                        m = d.bn_stats(a_stats[i][:, j, :], X[:, J * b + j, :])
                    m.then_inc(sa["a_stats"], 1)
                    d.wait_ge(sa["a_stats"], n)
                    wait("a_in", b - 1)
                    for j in range(J):
                        m = d.bn_aggr(a_mv[i][:, j, :], a_stats[i][:, j, :])
                    m.then_inc(sa["a_mv"], 1)

                def mid(b):
                    i, n = b % 2, b + 1
                    d.wait_ge(sa["wo"], n)
                    d.wait_ge(sa["a_in"], n)
                    wait("x12", b - 1)
                    d.scalar_tensor_tensor(out=x2[i][:, :, :].rearrange("p t d -> p (t d)"),
                                           in0=bank[4][:, :], scalar=0.5,
                                           in1=a_in[i][:, :, :].rearrange("p t d -> p (t d)"),
                                           op0=ALU.mult, op1=ALU.add).then_inc(sa["x2"], 1)
                    d.wait_ge(sa["x2"], n)
                    for j in range(J):
                        m = d.bn_stats(c_stats[i][:, j, :], x2[i][:, j, :])
                    m.then_inc(sa["c_stats"], 1)
                    d.wait_ge(sa["c_stats"], n)
                    wait("c_veps", b - 1)
                    for j in range(J):
                        m = d.bn_aggr(c_mv[i][:, j, :], c_stats[i][:, j, :])
                    m.then_inc(sa["c_mv"], 1)

                def norm_in(b):
                    i, n = b % 2, b + 1
                    d.wait_ge(sa["a_rstd"], n)
                    wait("h1Tp", b - 1)
                    for j in range(J):
                        m = d.tensor_scalar(h1[i][:, j, :], X[:, J * b + j, :], a_mv[i][:, j, 0:1],
                                            a_rstd[i][:, J + j:J + j + 1], ALU.subtract, ALU.mult)
                    m.then_inc(sa["a_norm"], 1)

                def norm_mid(b):
                    i, n = b % 2, b + 1
                    d.wait_ge(sa["c_rstd"], n)
                    wait("h2Tp", b - 1)
                    for j in range(J):
                        m = d.tensor_scalar(h2[i][:, j, :], x2[i][:, j, :], c_mv[i][:, j, 0:1],
                                            c_rstd[i][:, j:j + 1], ALU.subtract, ALU.mult)
                    m.then_inc(sa["h2"], 1)

                def peaks(b):
                    i, n = b % 2, b + 1
                    d.wait_ge(sa["k"], n)
                    if b == 0:
                        d.wait_ge(s_edge, 1)
                    wait("d_old", b - 1)
                    d.tensor_tensor_scan(peak[i][:, 1:T + 1], decay_row[:, :], bank[1][:, :], LOWEST,
                                         ALU.add, ALU.max).then_inc(sa["peak"], 1)

                def from_now(b):
                    i, n = b % 2, b + 1
                    d.wait_ge(sa["peak"], n)
                    d.tensor_tensor(d_now[i][:, :], bank[1][:, :], peak[i][:, 1:T + 1], ALU.subtract
                                    ).then_inc(sa["d_now"], 1)

                def from_out(b):
                    i, n = b % 2, b + 1
                    d.wait_ge(sa["peak"], n)
                    wait("den_old", b - 1)
                    wait("num_old", b - 1)
                    d.scalar_tensor_tensor(out=d_out[i][:, :], in0=bank[1][:, :],
                                           scalar=vec["time_first"][:, 0:1], in1=peak[i][:, 0:T],
                                           op0=ALU.add, op1=ALU.subtract).then_inc(sa["d_out"], 1)

                def mix_for_k(b):
                    i, n = b % 2, b + 1
                    d.wait_ge(sa["dh"], n)
                    wait("cwk", CC * (b - 1))
                    d.scalar_tensor_tensor(out=mix_k[i][:, :], in0=dh[i][:, :],
                                           scalar=vec["cm_mix_k"][:, 0:1], in1=h2T[i][:, 0:T],
                                           op0=ALU.mult, op1=ALU.add).then_inc(sa["mix_k"], 1)

                def mix_for_r(b):
                    i, n = b % 2, b + 1
                    d.wait_ge(sa["dh"], n)
                    wait("rr", b - 1)
                    d.scalar_tensor_tensor(out=mix_r[i][:, :], in0=dh[i][:, :],
                                           scalar=vec["cm_mix_r"][:, 0:1], in1=h2T[i][:, 0:T],
                                           op0=ALU.mult, op1=ALU.add).then_inc(sa["mix_r"], 1)

                def key_value(b):
                    i, n = b % 2, b + 1
                    d.wait_ge(sa["e2b"], n)
                    d.wait_ge(sa["v"], n)
                    d.tensor_tensor(kv[i][:, :], e2b[i][:, :], bank[2][:, :], ALU.mult
                                    ).then_inc(sa["kv"], 1)

                def scan_denominator(b):
                    i, n = b % 2, b + 1
                    d.wait_ge(sa["e2b"], n)
                    d.wait_ge(sa["e1b"], n)
                    wait("den_old", b - 1)
                    d.tensor_tensor_scan(bb[i][:, 1:T + 1], e1b[i][:, :], e2b[i][:, :], 0.0,
                                         ALU.mult, ALU.add).then_inc(sa["bb"], 1)

                def scan_numerator(b):
                    i, n = b % 2, b + 1
                    d.wait_ge(sa["kv"], n)
                    d.wait_ge(sa["e1b"], n)
                    wait("num_old", b - 1)
                    d.tensor_tensor_scan(aa[i][:, 1:T + 1], e1b[i][:, :], kv[i][:, :], 0.0,
                                         ALU.mult, ALU.add).then_inc(sa["aa"], 1)

                def new_numerator(b):
                    i, n = b % 2, b + 1
                    d.wait_ge(sa["e2"], n)
                    d.wait_ge(sa["v"], n)
                    wait("wo", b - 1)
                    d.tensor_tensor(num_new[i][:, :], e2[i][:, :], bank[2][:, :], ALU.mult
                                    ).then_inc(sa["num_new"], 1)

                def numerator(b):
                    i, n = b % 2, b + 1
                    d.wait_ge(sa["num_old"], n)
                    d.wait_ge(sa["num_new"], n)
                    d.tensor_tensor(num_new[i][:, :], num_new[i][:, :], num_old[i][:, :], ALU.add
                                    ).then_inc(sa["num"], 1)

                def invert(b):
                    i, n = b % 2, b + 1
                    d.wait_ge(sa["den"], n)
                    d.reciprocal(den_old[i][:, :], den_old[i][:, :]).then_inc(sa["rden"], 1)

                def receive(b):
                    i, n = b % 2, b + 1
                    d.wait_ge(sa["rden"], n)
                    d.wait_ge(sa["num"], n)
                    d.tensor_tensor(num_new[i][:, :], num_new[i][:, :], den_old[i][:, :], ALU.mult
                                    ).then_inc(sa["wkv"], 1)
                    d.wait_ge(sa["wkv"], n)
                    d.wait_ge(sa["th_r"], n)
                    d.scalar_tensor_tensor(out=rw[i][:, :], in0=th_r[i][:, :], scalar=1.0,
                                           in1=num_new[i][:, :], op0=ALU.add, op1=ALU.mult
                                           ).then_inc(sa["rw"], 1)

                def outputs(b):
                    i, n = b % 2, b + 1
                    d.wait_ge(sa["th_rr"], n)
                    d.wait_ge(sa["cwv"], n)
                    d.scalar_tensor_tensor(out=th_rr[i], in0=th_rr[i], scalar=1.0,
                                           in1=bank[5][:, :], op0=ALU.add, op1=ALU.mult
                                           ).then_inc(sa["rcv"], 1)
                    d.wait_ge(sa["rcv"], n)
                    d.wait_ge(sa["x12"], n)
                    d.scalar_tensor_tensor(out=flat(X, b), in0=th_rr[i], scalar=0.5,
                                           in1=flat(X, b), op0=ALU.mult, op1=ALU.add
                                           ).then_inc(sa["x_att"], 1)

                def norm_out(b):
                    norm_ffn(1, b)

                def scale_out(b):
                    scale_ffn(1, b)

                pipelined([(inputs, 0), (peaks, 1), (numerator, 2), (outputs, 5), (from_out, 1),
                           (norm_mid, 3), (from_now, 1), (invert, 2), (norm_in, 0), (mix_for_k, 3),
                           (receive, 2), (new_numerator, 1), (key_value, 1), (norm_out, 5),
                           (scan_denominator, 1), (scan_numerator, 1), (scale_out, 6), (mix_for_r, 3),
                           (mid, 2)])

            ffn(0)
            prepare()
            rwkv()
            ffn(1)
            add_moe(1)

        @block.tensor
        def _(t):
            t.wait_ge(s_const, 13)

            def keep_busy(times):
                for _ in range(times):
                    t.transpose(bank[6][:, 0:P], ident[:, :], ident[:, :])

            keep_busy(WARM_UP)
            t.wait_ge(s_wsh, 64)
            for c in range(SC):
                t.transpose(bank[2][:, c * P:c * P + P], w_gate_raw[:, c, :], ident[:, :])
                t.transpose(bank[3][:, c * P:c * P + P], w_up_raw[:, c, :], ident[:, :])
                t.transpose(bank[4][:, c * P:c * P + P], w_down_raw[:, c * P:c * P + P], ident[:, :])
            t.transpose(bank[5][:, 0:E], w_router_raw[:, :], ident[0:E, 0:E]).then_inc(s_wtp, 1)

            def turn(v, b):
                t.wait_ge(s_xn_d, v * NB + b + 1)
                t.wait_ge(s_xn_a, v * NB + b + 1)
                if v and b == 0:
                    t.wait_ge(sa["d_now"], NB)
                    t.wait_ge(sa["d_out"], NB)
                if v and b:
                    t.wait_ge(s_xnT, NB + b)
                if not v and b >= 2:
                    t.wait_ge(s_xnT, b - 1)
                for j in range(J):
                    m = t.transpose(bank[1 if v else b % 2][:, j * P:j * P + P], xn[:, J * b + j, :],
                                    ident[:, :])
                m.then_inc(s_xnTp, 1)

            def router(v, b):
                t.wait_ge(s_xnT, v * NB + b + 1)
                if v == 0 and b == 0:
                    t.wait_ge(s_wt, 1)
                if v and b == 0:
                    t.wait_ge(sa["pos_kk"], CC * NB)
                for j in range(J):
                    k = J * b + j
                    m = t.matmul(bank[7][:, k * E:k * E + E], xnT[:, b, j * P:j * P + P],
                                 w_routerT[:, :], start=True, stop=True)
                m.then_inc(s_logit, 1)

            def count_tokens(v):
                t.wait_ge(s_onehot, v + 1)
                oh = onehot[:, :, :].rearrange("p t e -> p (t e)")
                t.matmul(bank[0][:, 0:NT * E], ones[:, :], oh, start=True, stop=True)
                t.matmul(bank[1][:, 0:NT * E], before[:, :], oh, start=True, stop=True
                         ).then_inc(s_count, 1)

            def find_tokens(v):
                for t_ in range(NT):
                    if t_ % J == 0:
                        t.wait_ge(s_pos_hot, v * NB + t_ // J + 1)
                    m = t.matmul(bank[7][:, 0:2 * NBLK], pos_hot[:, t_, :],
                                 token_parts[:, t_, :, :].rearrange("p a b -> p (a b)"),
                                 start=(t_ == 0), stop=(t_ == NT - 1))
                m.then_inc(s_token, 1)

            def gate_up_chunk(v, b, c):
                n = (v * NB + b) * SC + c
                if 1 <= b <= BG:
                    t.wait_ge(s_up, (v * BG + b - 1) * SC + c + 1)
                elif n >= SC:
                    t.wait_ge(s_sact, n + 1 - SC)
                t.matmul(bank[2 + 2 * c][:, :], w_gateT[:, c, :], xnT[:, b, :], start=True, stop=True)
                t.matmul(bank[3 + 2 * c][:, :], w_upT[:, c, :], xnT[:, b, :], start=True, stop=True
                         ).then_inc(s_sgu, 1)

            def down_tiles(v, b):
                t.wait_ge(s_sact, (v * NB + b + 1) * SC)
                if v * NB + b:
                    t.wait_ge(s_sres, v * NB + b)
                for j in range(J):
                    for c in range(SC):
                        m = t.matmul(bank[6][:, j * P:j * P + P], act[c][:, j * P:j * P + P],
                                     w_downT[:, c, :], start=(c == 0), stop=(c == SC - 1))
                m.then_inc(s_sdn, 1)

            def shared(v):
                if v == 0:
                    gate_up_chunk(v, 0, 0)
                count_tokens(v)
                if v == 0:
                    gate_up_chunk(v, 0, 1)
                gate_up_chunk(v, 1, 0)
                down_tiles(v, 0)
                gate_up_chunk(v, 1, 1)
                find_tokens(v)
                gate_up_chunk(v, 2, 0)
                down_tiles(v, 1)
                gate_up_chunk(v, 2, 1)
                gate_up_chunk(v, 3, 0)
                down_tiles(v, 2)
                gate_up_chunk(v, 3, 1)
                down_tiles(v, 3)

            def moe(v):
                o = v * NBLK

                def turn_x(n, landed):
                    t.wait_ge(s_xb[n % NXB], landed)
                    t.transpose(bank[n % 2][:, 0:P], xb[n % NXB], ident[:, :]).then_inc(s_xbTp, 1)

                def gate_up_block(n, i, row):
                    t.wait_ge(s_xbT, i + (o + 1))
                    t.matmul(bank[2 + n % 2][:, :], xbT[n % 2][:, :], experts[:, bass.ds(row, F2)],
                             start=True, stop=True).then_inc(s_mgu, 1)

                def turn_a(n, i):
                    t.wait_ge(s_ma, i + (o + 1))
                    for c in range(FC):
                        m = t.transpose(bank[4 + n % 2][:, c * P:c * P + P], ma[n % 2][:, c * P:c * P + P],
                                        ident[:, :])
                    m.then_inc(s_maTp, 1)

                def down_block(n, i, row):
                    t.wait_ge(s_maT, i + (o + 1))
                    for c in range(FC):
                        m = t.matmul(bank[6 + n % 2][:, 0:P], maT[n % 2][:, c, :],
                                     experts[:, bass.ds(row + (F2 + c * D), D)],
                                     start=(c == 0), stop=(c == FC - 1))
                    m.then_inc(s_my, 1)

                def rows(i, n):
                    _, values = nc.values_load_multi_w_load_instructions(
                        block_row[0:1, bass.ds(i, n)], engines=[mybir.EngineType.PE],
                        min_val=0, max_val=(E - 1) * ROW,
                        skip_runtime_bounds_check_because="VectorE counted at most E - 1 experts")
                    return values

                def slot(i, row_down, row_up):
                    if i + 2 < NBLK:
                        turn_x(o + i + 2, 16 * ((o + i + 2) // NXB + 1))
                    if 0 <= i + 1 < NBLK:
                        gate_up_block(o + i + 1, i + 1, row_up)
                    if 0 <= i < NBLK:
                        turn_a(o + i, i)
                    if i == NBLK:
                        t.wait_ge(s_yb, o + i - 2)
                    if i == 1:
                        t.wait_ge(s_sres, (v + 1) * NB)
                    if 0 <= i - 1:
                        down_block(o + i - 1, i - 1, row_down)

                t.wait_ge(s_bexp, 3 * v + 3)
                t.wait_ge(s_rows, 3 * v + 3)
                if v == 0:
                    t.wait_ge(s_wmoe, 16 * (E // 4 + E))
                first = 2
                loops = (NBLK - 2 - first) // NXB
                row = rows(0, first + 1)
                for i in range(-2, first):
                    slot(i, row[max(i - 1, 0)], row[max(i + 1, 0)])
                with t.Fori(0, loops) as r:
                    for k in range(NXB):
                        i = r * NXB + (first + k)
                        n = o + first + k
                        if k % 4 == 0:
                            row = rows(i - 1, 6)
                        turn_x(n + 2, r * 16 + 16 * ((n + 2) // NXB + 1))
                        gate_up_block(n + 1, i + 1, row[k % 4 + 2])
                        turn_a(n, i)
                        down_block(n - 1, i - 1, row[k % 4])
                start = first + loops * NXB
                for i in range(start, NBLK + 1):
                    if (i - start) % 4 == 0:
                        row = rows(i - 1, min(6, NBLK - i + 1))
                    k = (i - start) % 4
                    slot(i, row[k], row[k + 2] if i + 1 < NBLK else None)

            def ffn(v):
                if v == 0:
                    keep_busy(WARM)
                    turn(v, 0)
                    keep_busy(WARM)
                    turn(v, 1)
                    keep_busy(WARM)
                    router(v, 0)
                    turn(v, 2)
                    router(v, 1)
                    turn(v, 3)
                    router(v, 2)
                    router(v, 3)
                shared(v)
                moe(v)

            def rwkv():
                def wait(name, n):
                    if n > 0:
                        t.wait_ge(sa[name], n)

                def turn_rows(b, src, name):
                    for j in range(J):
                        m = t.transpose(bank[0][:, j * P:j * P + P], src[b % 2][:, j, :], ident[:, :])
                    m.then_inc(sa[name], 1)

                def turn_in(b):
                    t.wait_ge(sa["a_norm"], b + 1)
                    if b == 0:
                        t.wait_ge(s_yb, NBLK)
                    wait("h1T", b)
                    wait("h2T", b - 2)
                    turn_rows(b, h1, "h1Tp")

                def turn_mid(b):
                    t.wait_ge(sa["h2"], b + 1)
                    wait("h1T", min(b + 3, NB))
                    wait("h2T", b)
                    turn_rows(b, h2, "h2Tp")

                def product(b, m, bank_, readers):
                    i = b % 2
                    t.wait_ge(sa["h1T"], b + 1)
                    if b == 0:
                        t.wait_ge(s_wmix, 1)
                    for name in readers:
                        wait(name, b)
                    t.matmul(bank_[:, :], w_now[m][:, :], h1T[i][:, 1:T + 1], start=True, stop=False)
                    t.matmul(bank_[:, :], w_prev[m][:, :], h1T[i][:, 0:T], start=False, stop=True
                             ).then_inc(sa[m], 1)

                def key(b):
                    product(b, "k", bank[1], ("d_now", "d_out"))

                def value(b):
                    product(b, "v", bank[2], ("kv", "num_new"))

                def reception(b):
                    product(b, "r", bank[3], ("th_r",))

                def channel(b, c0):
                    t.wait_ge(sa["mix_k"], b + 1)
                    for c in range(c0, c0 + 2):
                        wait("pos_kk", CC * b + c - 1)
                        t.matmul(bank[6 + c % 2][:, :], cwk[:, c * P:c * P + P], mix_k[b % 2][:, :],
                                 start=True, stop=True).then_inc(sa["cwk"], 1)

                def first_channels(b):
                    channel(b, 0)

                def last_channels(b):
                    channel(b, 2)

                def channel_gate(b):
                    t.wait_ge(sa["mix_r"], b + 1)
                    wait("x2", min(b + 2, NB))
                    wait("th_rr", b)
                    for j in range(J):
                        m = t.matmul(bank[4][:, j * P:j * P + P], mix_r[b % 2][:, j * P:j * P + P],
                                     cwr[:, :], start=True, stop=True)
                    m.then_inc(sa["rr"], 1)

                def channel_out(b):
                    t.wait_ge(sa["kk"], CC * (b + 1))
                    wait("rcv", b)
                    for j in range(J):
                        for c in range(CC):
                            m = t.matmul(bank[5][:, j * P:j * P + P], kk[c][:, j * P:j * P + P],
                                         cwv[:, c, :], start=(c == 0), stop=(c == CC - 1))
                    m.then_inc(sa["cwv"], 1)

                def project(b):
                    t.wait_ge(sa["rw"], b + 1)
                    wait("x2", b)
                    wait("th_rr", b - 1)
                    for j in range(J):
                        m = t.matmul(bank[4][:, j * P:j * P + P], rw[b % 2][:, j * P:j * P + P], wo[:, :],
                                     start=True, stop=True)
                    m.then_inc(sa["wo"], 1)

                def turn_out(b):
                    turn(1, b)

                def router_out(b):
                    router(1, b)

                def shared_out(c):
                    if c < SC:
                        for name in (("kv", "num_new", "th_r"), ("x2", "th_rr", "rcv"))[c]:
                            t.wait_ge(sa[name], NB)
                        gate_up_chunk(1, 0, c)

                pipelined([(turn_in, 0), (first_channels, 3), (project, 2), (key, 0),
                           (last_channels, 3), (router_out, 8), (channel_gate, 3), (value, 0),
                           (turn_mid, 2), (turn_out, 7), (shared_out, 8), (reception, 0), (channel_out, 3)])

            ffn(0)
            rwkv()
            ffn(1)


_INS = ["L0_attn_x", "L0_attn_ln1_g", "L0_attn_ln1_b", "L0_attn_ln2_g", "L0_attn_ln2_b",
        "L0_attn_tm_mix_k", "L0_attn_tm_mix_v", "L0_attn_tm_mix_r", "L0_attn_time_decay",
        "L0_attn_time_first", "L0_attn_wk", "L0_attn_wv", "L0_attn_wr", "L0_attn_wo",
        "L0_attn_cm_mix_k", "L0_attn_cm_mix_r", "L0_attn_cwk", "L0_attn_cwv", "L0_attn_cwr",
        "L0_ffn_w_router", "L0_ffn_gate_up_proj", "L0_ffn_down_proj", "L0_ffn_w_gate",
        "L0_ffn_w_up", "L0_ffn_w_down"]


def kernel(**inputs):
    import numpy as _np
    import concourse.bacc as _bacc
    from concourse import mybir as _mybir
    from concourse.bass_utils import run_bass_kernel_spmd as _run

    nc = _bacc.Bacc("TRN2", target_bir_lowering=False, num_devices=1)
    arrays, args = {}, {}
    for name in _INS:
        a = _np.ascontiguousarray(inputs[name])
        arrays[f"in_{name}_dram"] = a
        args[name] = nc.dram_tensor(f"in_{name}_dram", a.shape, _mybir.dt.from_np(a.dtype),
                                    kind="ExternalInput").ap()
    shape = inputs["L0_attn_x"].shape
    out = nc.dram_tensor("out_0_dram", shape, _mybir.dt.float32, kind="ExternalOutput").ap()
    macaron_kernel(nc, args, out)
    r = _run(nc, [arrays], core_ids=[0])
    return r.results[0]["out_0_dram"]
```
